# Optimizing a Trainium2 kernel written in Bass

```python
import numpy as np
import jax
import jax.numpy as jnp

def _softmax(x, axis=-1):
    return jax.nn.softmax(x, axis=axis)

def _gelu(x):
    return jax.nn.gelu(x, approximate=True)

def _silu(x):
    return jax.nn.silu(x)

def _sigmoid(x):
    return jax.nn.sigmoid(x)

def _layernorm(x, axis=-1, eps=1e-05):
    m = jnp.mean(x, axis=axis, keepdims=True)
    v = jnp.var(x, axis=axis, keepdims=True)
    return (x - m) / jnp.sqrt(v + eps)

def _scatter_add(tgt, idx, src, axis=0):
    return tgt.at[idx].add(src)

def _segment_sum(src, seg, n):
    return jax.ops.segment_sum(src, seg, n)
kernel_name = 'mk_lm_tower_d1_tok_ids1024_r4_af2e3e'

def setup_inputs(seed: int=0):
    np.random.seed(seed)
    _w = jnp.asarray

    def _rec_inputs():
        import jax
        import jax.numpy as jnp
        _rk = jax.random.key(seed)
        x = jax.random.randint(jax.random.fold_in(_rk, 1), (16, 256), 0, 12564, jnp.int32)
        return x
    x = _rec_inputs()

    def _L0_tok_setup():
        import jax, jax.numpy as jnp
        import numpy as np
        NUM_EMBEDDINGS = 50257
        EMBEDDING_DIM = 256
        key = jax.random.key(seed)
        k_x, k_w = jax.random.split(key)
        x = jax.random.randint(k_x, (8, 512), 0, NUM_EMBEDDINGS, dtype=jnp.int32)
        w = jax.random.normal(k_w, (NUM_EMBEDDINGS, EMBEDDING_DIM), dtype=jnp.float32)
        return {'x': x, 'w': w}
    _L0_tok_all = _L0_tok_setup()
    _L0_tok_in = {k: v for k, v in _L0_tok_all.items() if k in ('w',)}
    del _L0_tok_all

    def _L0_attn_setup():
        import jax, jax.numpy as jnp
        import numpy as np
        B, T, D = (2, 512, 256)
        HEAD_DIM, N_HEADS, N_HH, HEAD_V_DIM, CONV_SIZE = (128, 8, 3, 128, 4)

        def _short_conv(x, w):
            cs = w.shape[-1]
            t = x.shape[1]
            xp = jnp.pad(x, ((0, 0), (cs - 1, 0), (0, 0)))
            y = sum((xp[:, i:i + t, :] * w[:, i] for i in range(cs)))
            return jax.nn.silu(y)

        def _l2norm(x, eps=1e-06):
            return x * jax.lax.rsqrt(jnp.sum(x * x, -1, keepdims=True) + eps)

        def _forward(x, Wq, Wk, Wv, Wb, Wa, A_log, dt_bias, conv_q, conv_k, conv_v, Wg, rms_weight, Wo):
            b, t, _ = x.shape
            h, d, dv, nh = (N_HEADS, HEAD_DIM, HEAD_V_DIM, N_HH)
            q = _short_conv(x @ Wq, conv_q).reshape(b, t, h, d)
            k = _short_conv(x @ Wk, conv_k).reshape(b, t, nh, h, d).transpose(0, 1, 3, 2, 4)
            v = _short_conv(x @ Wv, conv_v).reshape(b, t, nh, h, dv).transpose(0, 1, 3, 2, 4)
            beta = 2.0 * jax.nn.sigmoid(x @ Wb).reshape(b, t, nh, h).transpose(0, 1, 3, 2)
            g = -jnp.exp(A_log) * jax.nn.softplus(x @ Wa + dt_bias)
            q = _l2norm(q) * d ** (-0.5)
            k = _l2norm(k)

            def step(S, inp):
                qt, kt, vt, bt, gt = inp
                S = S * jnp.exp(gt)[..., None, None]
                for i in range(nh):
                    ki, vi, bi = (kt[:, :, i], vt[:, :, i], bt[:, :, i])
                    kS = jnp.einsum('bhd,bhde->bhe', ki, S)
                    S = S + bi[..., None, None] * (ki[..., None] * (vi - kS)[:, :, None, :])
                o = jnp.einsum('bhd,bhde->bhe', qt, S)
                return (S, o)
            xs = tuple((jnp.moveaxis(a, 1, 0) for a in (q, k, v, beta, g)))
            S0 = jnp.zeros((b, h, d, dv), x.dtype)
            _, o = jax.lax.scan(step, S0, xs)
            o = jnp.moveaxis(o, 0, 1)
            gate = (x @ Wg).reshape(b, t, h, dv)
            o = o * jax.lax.rsqrt(jnp.mean(o * o, -1, keepdims=True) + 1e-05) * rms_weight
            o = o * jax.nn.silu(gate)
            return o.reshape(b, t, h * dv) @ Wo
        key = jax.random.key(seed)
        ks = jax.random.split(key, 16)
        h, d, dv, nh, cs = (N_HEADS, HEAD_DIM, HEAD_V_DIM, N_HH, CONV_SIZE)
        f = lambda k, shape, s=0.02: jax.random.normal(k, shape, jnp.float32) * s
        return {'x': f(ks[0], (B, T, D), 1.0), 'cos': f(ks[1], (T, d), 1.0), 'sin': f(ks[2], (T, d), 1.0), 'Wq': f(ks[3], (D, h * d)), 'Wk': f(ks[4], (D, h * d * nh)), 'Wv': f(ks[5], (D, h * dv * nh)), 'Wb': f(ks[6], (D, h * nh)), 'Wa': f(ks[7], (D, h)), 'A_log': jnp.log(jax.random.uniform(ks[8], (h,), jnp.float32, 0.5, 8.0)), 'dt_bias': f(ks[9], (h,), 0.1), 'conv_q': f(ks[10], (h * d, cs), 0.5), 'conv_k': f(ks[11], (h * d * nh, cs), 0.5), 'conv_v': f(ks[12], (h * dv * nh, cs), 0.5), 'Wg': f(ks[13], (D, h * dv)), 'rms_weight': jnp.ones((dv,), jnp.float32), 'Wo': f(ks[14], (h * dv, D))}
    _L0_attn_all = _L0_attn_setup()
    _L0_attn_in = {k: v for k, v in _L0_attn_all.items() if k in ('cos', 'sin', 'Wq', 'Wk', 'Wv', 'Wb', 'Wa', 'A_log', 'dt_bias', 'conv_q', 'conv_k', 'conv_v', 'Wg', 'rms_weight', 'Wo')}
    del _L0_attn_all

    def _L0_ffn_setup():
        import math
        import jax, jax.numpy as jnp
        import numpy as np
        NUM_EXPERTS = 8
        CAPACITY_FACTOR = 1.5
        key = jax.random.key(seed)
        ks = jax.random.split(key, 4)
        B, T, D, F, E = (4, 512, 256, 1024, NUM_EXPERTS)
        scale = 0.02
        return {'x': jax.random.normal(ks[0], (B, T, D), dtype=jnp.float32), 'router_w': jax.random.normal(ks[1], (E, D), dtype=jnp.float32) * scale, 'w1': jax.random.normal(ks[2], (E, D, F), dtype=jnp.float32) * scale, 'b1': jnp.zeros((E, F), dtype=jnp.float32), 'w2': jax.random.normal(ks[3], (E, F, D), dtype=jnp.float32) * scale, 'b2': jnp.zeros((E, D), dtype=jnp.float32)}
    _L0_ffn_all = _L0_ffn_setup()
    _L0_ffn_in = {k: v for k, v in _L0_ffn_all.items() if k in ('router_w', 'w1', 'b1', 'w2', 'b2')}
    del _L0_ffn_all
    return {'x': x, 'L0_tok_w': _L0_tok_in['w'], 'L0_attn_cos': _L0_attn_in['cos'], 'L0_attn_sin': _L0_attn_in['sin'], 'L0_attn_Wq': _L0_attn_in['Wq'], 'L0_attn_Wk': _L0_attn_in['Wk'], 'L0_attn_Wv': _L0_attn_in['Wv'], 'L0_attn_Wb': _L0_attn_in['Wb'], 'L0_attn_Wa': _L0_attn_in['Wa'], 'L0_attn_A_log': _L0_attn_in['A_log'], 'L0_attn_dt_bias': _L0_attn_in['dt_bias'], 'L0_attn_conv_q': _L0_attn_in['conv_q'], 'L0_attn_conv_k': _L0_attn_in['conv_k'], 'L0_attn_conv_v': _L0_attn_in['conv_v'], 'L0_attn_Wg': _L0_attn_in['Wg'], 'L0_attn_rms_weight': _L0_attn_in['rms_weight'], 'L0_attn_Wo': _L0_attn_in['Wo'], 'L0_ffn_router_w': _L0_ffn_in['router_w'], 'L0_ffn_w1': _L0_ffn_in['w1'], 'L0_ffn_b1': _L0_ffn_in['b1'], 'L0_ffn_w2': _L0_ffn_in['w2'], 'L0_ffn_b2': _L0_ffn_in['b2']}

def reference(x, L0_tok_w, L0_attn_cos, L0_attn_sin, L0_attn_Wq, L0_attn_Wk, L0_attn_Wv, L0_attn_Wb, L0_attn_Wa, L0_attn_A_log, L0_attn_dt_bias, L0_attn_conv_q, L0_attn_conv_k, L0_attn_conv_v, L0_attn_Wg, L0_attn_rms_weight, L0_attn_Wo, L0_ffn_router_w, L0_ffn_w1, L0_ffn_b1, L0_ffn_w2, L0_ffn_b2):
    import jax
    import jax.numpy as jnp

    def _L0_tok_ref(x, w):
        import jax, jax.numpy as jnp
        import numpy as np
        NUM_EMBEDDINGS = 50257
        EMBEDDING_DIM = 256
        return jnp.take(w, x, axis=0)

    def _L0_attn_ref(x, cos, sin, Wq, Wk, Wv, Wb, Wa, A_log, dt_bias, conv_q, conv_k, conv_v, Wg, rms_weight, Wo):
        import jax, jax.numpy as jnp
        import numpy as np
        B, T, D = (2, 512, 256)
        HEAD_DIM, N_HEADS, N_HH, HEAD_V_DIM, CONV_SIZE = (128, 8, 3, 128, 4)

        def _short_conv(x, w):
            cs = w.shape[-1]
            t = x.shape[1]
            xp = jnp.pad(x, ((0, 0), (cs - 1, 0), (0, 0)))
            y = sum((xp[:, i:i + t, :] * w[:, i] for i in range(cs)))
            return jax.nn.silu(y)

        def _l2norm(x, eps=1e-06):
            return x * jax.lax.rsqrt(jnp.sum(x * x, -1, keepdims=True) + eps)

        def _forward(x, Wq, Wk, Wv, Wb, Wa, A_log, dt_bias, conv_q, conv_k, conv_v, Wg, rms_weight, Wo):
            b, t, _ = x.shape
            h, d, dv, nh = (N_HEADS, HEAD_DIM, HEAD_V_DIM, N_HH)
            q = _short_conv(x @ Wq, conv_q).reshape(b, t, h, d)
            k = _short_conv(x @ Wk, conv_k).reshape(b, t, nh, h, d).transpose(0, 1, 3, 2, 4)
            v = _short_conv(x @ Wv, conv_v).reshape(b, t, nh, h, dv).transpose(0, 1, 3, 2, 4)
            beta = 2.0 * jax.nn.sigmoid(x @ Wb).reshape(b, t, nh, h).transpose(0, 1, 3, 2)
            g = -jnp.exp(A_log) * jax.nn.softplus(x @ Wa + dt_bias)
            q = _l2norm(q) * d ** (-0.5)
            k = _l2norm(k)

            def step(S, inp):
                qt, kt, vt, bt, gt = inp
                S = S * jnp.exp(gt)[..., None, None]
                for i in range(nh):
                    ki, vi, bi = (kt[:, :, i], vt[:, :, i], bt[:, :, i])
                    kS = jnp.einsum('bhd,bhde->bhe', ki, S)
                    S = S + bi[..., None, None] * (ki[..., None] * (vi - kS)[:, :, None, :])
                o = jnp.einsum('bhd,bhde->bhe', qt, S)
                return (S, o)
            xs = tuple((jnp.moveaxis(a, 1, 0) for a in (q, k, v, beta, g)))
            S0 = jnp.zeros((b, h, d, dv), x.dtype)
            _, o = jax.lax.scan(step, S0, xs)
            o = jnp.moveaxis(o, 0, 1)
            gate = (x @ Wg).reshape(b, t, h, dv)
            o = o * jax.lax.rsqrt(jnp.mean(o * o, -1, keepdims=True) + 1e-05) * rms_weight
            o = o * jax.nn.silu(gate)
            return o.reshape(b, t, h * dv) @ Wo
        return _forward(x, Wq, Wk, Wv, Wb, Wa, A_log, dt_bias, conv_q, conv_k, conv_v, Wg, rms_weight, Wo)

    def _L0_ffn_ref(x, router_w, w1, b1, w2, b2):
        import math
        import jax, jax.numpy as jnp
        import numpy as np
        NUM_EXPERTS = 8
        CAPACITY_FACTOR = 1.5
        B, T, D = x.shape
        E = router_w.shape[0]
        N = B * T
        C = max(math.ceil(CAPACITY_FACTOR * N / E), 1)
        x_flat = x.reshape(N, D)
        logits = x_flat @ router_w.T
        probs = jax.nn.softmax(logits, axis=-1)
        chosen_e = jnp.argmax(probs, axis=-1)
        chosen_p = jnp.max(probs, axis=-1)
        onehot = jax.nn.one_hot(chosen_e, E, dtype=jnp.float32)
        pos = jnp.take_along_axis(jnp.cumsum(onehot, axis=0), chosen_e[:, None], axis=1)[:, 0] - 1.0
        pos = pos.astype(jnp.int32)
        kept = pos < C
        pos_c = jnp.clip(pos, 0, C - 1)
        buf = jnp.zeros((E, C, D), dtype=x.dtype).at[chosen_e, pos_c].add(x_flat * kept[:, None].astype(x.dtype))
        h = jax.nn.gelu(jnp.einsum('ecd,edf->ecf', buf, w1) + b1[:, None, :], approximate=False)
        eo = jnp.einsum('ecf,efd->ecd', h, w2) + b2[:, None, :]
        y = eo[chosen_e, pos_c] * (chosen_p * kept.astype(x.dtype))[:, None]
        return y.reshape(B, T, D)
    h = _L0_tok_ref(x, L0_tok_w)
    h = h + _L0_attn_ref(_layernorm(h, axis=-1), L0_attn_cos, L0_attn_sin, L0_attn_Wq, L0_attn_Wk, L0_attn_Wv, L0_attn_Wb, L0_attn_Wa, L0_attn_A_log, L0_attn_dt_bias, L0_attn_conv_q, L0_attn_conv_k, L0_attn_conv_v, L0_attn_Wg, L0_attn_rms_weight, L0_attn_Wo)
    h = h + _L0_ffn_ref(_layernorm(h, axis=-1), L0_ffn_router_w, L0_ffn_w1, L0_ffn_b1, L0_ffn_w2, L0_ffn_b2)
    return h

_drawn_inputs = setup_inputs


def setup_inputs(seed=0):
    import zlib

    import numpy as np

    out = dict(_drawn_inputs(seed))
    spreads = {'L0_attn_rms_weight': (1.0, 0.6), 'L0_ffn_b1': (0.0, 0.8), 'L0_ffn_b2': (0.0, 0.405)}
    factors = {'L0_attn_Wb': 6.601, 'L0_attn_Wa': 8.0, 'L0_attn_A_log': 2.82, 'L0_attn_dt_bias': 32.009}
    for name, (base, spread) in spreads.items():
        noise = np.random.default_rng([zlib.crc32(name.encode()), seed]).standard_normal(out[name].shape)
        drawn = base * np.exp(spread * noise) if base else spread * noise
        out[name] = jnp.asarray(drawn.astype(out[name].dtype))
    for name, factor in factors.items():
        out[name] = (out[name] * factor).astype(out[name].dtype)
    return out
```

```python
from contextlib import ExitStack

import concourse.bass as bass
from concourse import mybir

ALU = mybir.AluOpType
ACT = mybir.ActivationFunctionType
F32 = mybir.dt.float32
BF16 = mybir.dt.bfloat16
I32 = mybir.dt.int32
AX_X = mybir.AxisListType.X
P = 128

B, T, D = 16, 256, 256
N = B * T
H, HD, NH, CS = 8, 128, 3, 4
KD_ = D // P
E, F = 8, 1024
CAP = -(-3 * N // (2 * E))
C = 32
NC_ = T // C
R = NH * C
CB = B * C
IT = H * NC_
LEVELS = 5
TT = 2 * NH + 1
QT = NH
GATE = TT
G_MIN = -104.0
LN_EPS, L2_EPS, RMS_EPS = 1e-5, 1e-6, 1e-5
NT = N // P
TRASH = E * CAP

STREAM = [("kn", 0), ("d", 0), ("kn", 1), ("e", 0), ("c", 0), ("kn", 2), ("c", 1), ("kn", 3),
          ("c", 2), ("vn", 0), ("c", 3), ("vn", 1), ("c", 4), ("vn", 2), ("c", 5), ("vn", 3),
          ("c", 6), ("g", 0)]
FIRST = [s for s in STREAM if s[0] in "decg"]
N0, NS = len(FIRST), len(STREAM)
N_AFTER = [(1, 1), (1, 1), (1, 1), (1, 1), (1, 0)]


def build(nc, x, w_tok, wq, wk, wv, wb, wa, a_log, dt_bias, conv_q, conv_k, conv_v, wg,
          rms_weight, wo, router_w, w1, b1, w2, b2, out):
    with ExitStack() as ctx:
        def sem(name):
            return ctx.enter_context(nc.semaphore(name))

        h_dram = nc.dram_tensor("h_dram", [N, D], F32, kind="Internal").ap()
        o_dram = nc.dram_tensor("o_dram", [H, P, B, T], F32, kind="Internal").ap()
        xe_dram = nc.dram_tensor("xe_dram", [TRASH + N, D], F32, kind="Internal").ap()
        ye_dram = nc.dram_tensor("ye_dram", [TRASH, D], F32, kind="Internal").ap()

        ident = ctx.enter_context(nc.sbuf_tensor("ident", [P, P], F32))
        with ExitStack() as attn:
            def sb(name, shape, dt=F32):
                return attn.enter_context(nc.sbuf_tensor(name, shape, dt))
            t = {}
            t["xnT"] = sb("xnT", [P, KD_, NC_, CB])
            t["glog"] = sb("glog", [C, (IT + 1) * B])
            t["beta"] = sb("beta", [R, IT * B])
            t["neg_eg"] = sb("neg_eg", [R, IT * B])
            t["keep"] = sb("keep", [P, IT + 1])
            t["start"] = sb("start", [P, IT + 1])
            t["tri"] = sb("tri", [C, C])
            t["suf3"] = sb("suf3", [C, R])
            t["ones"] = sb("ones", [P, P])
            t["one_d"] = sb("one_d", [P, P])
            t["eps_d"] = sb("eps_d", [P, P])
            t["dmask"] = sb("dmask", [R, NH + 1, C])
            t["mask0"] = sb("mask0", [R, R])
            t["lmask"] = sb("lmask", [R, LEVELS, R // 2])
            t["eps_rms"] = sb("eps_rms", [P, 1])
            embed(nc, t, ident, x, w_tok, wb, wa, a_log, dt_bias, h_dram, xe_dram, sem)
            attention(nc, t, ident, wq, wk, wv, wg, conv_q, conv_k, conv_v, o_dram, sem)
        k = {"h2": ctx.enter_context(nc.sbuf_tensor("h2", [P, NT, D], F32)),
             "weight": ctx.enter_context(nc.sbuf_tensor("weight", [P, NT], F32)),
             "slot": ctx.enter_context(nc.sbuf_tensor("slot_of", [P, NT], I32))}
        project_and_route(nc, k, ident, wo, rms_weight, router_w, h_dram, o_dram, xe_dram, sem)
        experts(nc, ident, w1, b1, w2, b2, xe_dram, ye_dram, sem)
        combine(nc, k, ye_dram, out, sem)


def embed(nc, t, ident, x, w_tok, wb, wa, a_log, dt_bias, h_dram, xe_dram, sem):
    QN = 4
    QT_ = NT // QN
    with ExitStack() as ctx:
        def sb(name, shape, dt=F32):
            return ctx.enter_context(nc.sbuf_tensor(name, shape, dt))
        ids = sb("ids", [P, NT], I32)
        rows = sb("rows", [P, NT, D])
        xn = sb("xn", [P, NT, D])
        sq = sb("sq", [P, QT_, D])
        stat = sb("stat", [P, 4, NT])
        eps_ln = sb("eps_ln", [P, 1])
        zrow = sb("zrow", [P, CAP * E // P // 4, D])
        wab = sb("wab", [P, KD_, C])
        gates = xn[0:C, 0:16, :].rearrange("p a b -> p (a b)")
        gatesT = xn[0:C, 16:32, :].rearrange("p a b -> p (a b)")
        gt3 = gatesT.rearrange("p (m ch) -> p m ch", ch=C)
        tri3 = sb("tri3", [C, R])
        dtb = sb("dtb", [C, H])
        alog = sb("alog", [C, H])
        expa = sb("expa", [C, H])
        one32 = sb("one32", [C, 1])
        soft = sb("soft", [C, 5, H * P])
        lm = sb("lm", [C, LEVELS, R // 2])
        dm = sb("dm", [C, NH, NH + 1, C])
        m0 = sb("m0", [C, NH, R])
        pt = ctx.enter_context(nc.psum_tensor("pt", [P, 4, 512], F32))
        pg = ctx.enter_context(nc.psum_tensor("pg", [P, 2, 512], F32))

        s_ids = sem("e_ids")
        s_small = sem("e_small")
        s_rows = [sem(f"e_rows{q}") for q in range(QN)]
        s_hstore = sem("e_hstore")
        s_zero = sem("e_zero")
        s_cst = sem("e_cst")
        s_v = sem("e_v")
        s_cent = sem("e_cent")
        s_sq = sem("e_sq")
        s_var = sem("e_var")
        s_sd = sem("e_sd")
        s_xn = sem("e_xn")
        s_tr = sem("e_tr")
        s_xt = sem("e_xt")
        s_g = sem("e_g")
        s_gc = sem("e_gc")
        s_gv = sem("e_gv")
        s_ga = sem("e_ga")
        s_eg = sem("e_eg")
        s_lm = sem("e_lm")
        xv = t["xnT"].rearrange("p k c (b t) -> p k c b t", b=B)
        n_gl = H * P

        block = ctx.enter_context(nc.Block())

        @block.sync
        def _(sp):
            sp.dma_start(ids[:, :], x.rearrange("b (s p) -> p (b s)", p=P),
                         allow_slow_non_contiguous=True).then_inc(s_ids, 16)
            for k in range(KD_):
                sp.dma_start(wab[:, k, 0:H * NH], wb[k * P:(k + 1) * P, :]).then_inc(s_small, 16)
                sp.dma_start(wab[:, k, H * NH:], wa[k * P:(k + 1) * P, :]).then_inc(s_small, 16)
            sp.dma_start(dtb[:, :], dt_bias.unsqueeze(0).to_broadcast([C, H])).then_inc(s_small, 16)
            sp.dma_start(alog[:, :], a_log.unsqueeze(0).to_broadcast([C, H])).then_inc(s_small, 16)
            for q in range(QN):
                sp.wait_ge(s_rows[q], 16 * QT_)
                sp.dma_start(h_dram[q * QT_ * P:(q + 1) * QT_ * P, :].rearrange("(j p) d -> p j d", p=P),
                             rows[:, q * QT_:(q + 1) * QT_, :]).then_inc(s_hstore, 16)
            sp.wait_ge(s_zero, 1)
            for q in range(4):
                n = CAP * E // 4
                sp.dma_start(xe_dram[q * n:(q + 1) * n, :].rearrange("(p j) d -> p j d", p=P),
                             zrow[:, :, :]).then_inc(s_hstore, 16)
            sp.wait_ge(s_hstore, 16 * (QN + 4))

        @block.gpsimd
        def _(pool):
            pool.wait_ge(s_ids, 16)
            for j in range(NT):
                pool.indirect_dma_start(rows[:, j, :], None, w_tok,
                                        bass.IndirectOffsetOnAxis(ap=ids[:, j:j + 1], axis=0)
                                        ).then_inc(s_rows[j // QT_], 16)
            cnt = [0]

            def step(ins):
                cnt[0] += 1
                ins.then_inc(s_cst, 1)
                pool.wait_ge(s_cst, cnt[0])

            def sel(ap, pattern, base, cm, op):
                step(pool.affine_select(out=ap, in_=ap, compare_op=op, fill=0.0, base=base,
                                        pattern=pattern, channel_multiplier=cm))

            step(pool.memset(ident[:, :], 1.0))
            sel(ident[:, :], [[-1, P]], 0, 1, ALU.is_equal)
            step(pool.memset(t["tri"][:, :], 1.0))
            sel(t["tri"][:, :], [[1, C]], 0, -1, ALU.is_ge)
            step(pool.memset(tri3[:, :], 1.0))
            sel(tri3[:, :], [[0, NH], [1, C]], 0, -1, ALU.is_ge)
            step(pool.memset(t["suf3"][:, :], 1.0))
            sel(t["suf3"][:, :], [[0, NH], [-1, C]], 0, 1, ALU.is_gt)
            step(pool.memset(lm[:, :, :], 1.0))
            for lev in range(LEVELS):
                w = 1 << lev
                nb = C // (2 * w)
                sel(lm[:, lev, :], [[0, NH], [-2 * w, nb], [0, w]], -w, 1, ALU.is_ge)
                sel(lm[:, lev, :], [[0, NH], [2 * w, nb], [0, w]], 2 * w - 1, -1, ALU.is_ge)
            step(pool.memset(dm[:, :, 0:NH, :], -1.0))
            step(pool.memset(dm[:, :, NH, :], 1.0))
            step(pool.memset(m0[:, :, :], 0.0))
            for i in range(NH):
                sel(dm[:, i, 0:i + 1, :], [[0, i + 1], [1, C]], 0, -1, ALU.is_gt)
                sel(dm[:, i, i + 1:, :], [[0, NH - i], [1, C]], 0, -1, ALU.is_ge)
                if i < NH - 1:
                    later = m0[:, i, C * (i + 1):]
                    step(pool.memset(later, 1.0))
                    sel(later, [[0, NH - 1 - i], [1, C]], 0, -1, ALU.is_equal)
            pool.drain().then_inc(s_lm, 1)

        @block.vector
        def _(dve):
            done = [0]

            def step(ins):
                done[0] += 1
                ins.then_inc(s_v, 1)
                dve.wait_ge(s_v, done[0])

            dve.memset(zrow[:, :, :], 0.0).then_inc(s_zero, 1)
            step(dve.memset(eps_ln[:, :], LN_EPS))
            step(dve.memset(one32[:, :], 1.0))
            dve.memset(t["ones"][:, :], 1.0)
            dve.memset(t["one_d"][:, :], 1.0 / HD)
            dve.memset(t["eps_d"][:, :], RMS_EPS * HD)
            dve.memset(t["eps_rms"][:, :], RMS_EPS * HD * L2_EPS)
            step(dve.memset(t["keep"][:, :], 1.0))
            step(dve.memset(t["start"][:, :], 0.0))
            dve.memset(t["keep"][:, ::NC_], 0.0)
            dve.memset(t["start"][:, ::NC_], -1e30)
            dve.memset(t["glog"][:, IT * B:], 0.0)
            for q in range(QN):
                qs = slice(q * QT_, (q + 1) * QT_)
                dve.wait_ge(s_rows[q], 16 * QT_)
                step(dve.tensor_reduce(stat[:, 0, qs], rows[:, qs, :], AX_X, ALU.add))
                step(dve.tensor_scalar(stat[:, 0, qs], stat[:, 0, qs], -1.0 / D, None, ALU.mult))
                step(dve.tensor_tensor(xn[:, qs, :], rows[:, qs, :],
                                       stat[:, 0, qs].unsqueeze(2).to_broadcast([P, QT_, D]), ALU.add))
                dve.tensor_scalar(stat[:, 2, qs], stat[:, 0, qs], 0.0, None, ALU.mult).then_inc(s_cent, 1)
                dve.wait_ge(s_sq, q + 1)
                dve.tensor_reduce(stat[:, 1, qs], sq[:, :, :], AX_X, ALU.add).then_inc(s_var, 1)
                dve.wait_ge(s_sd, q + 1)
                step(dve.reciprocal(stat[:, 3, qs], stat[:, 2, qs]))
                dve.tensor_tensor(xn[:, qs, :], xn[:, qs, :],
                                  stat[:, 3, qs].unsqueeze(2).to_broadcast([P, QT_, D]),
                                  ALU.mult).then_inc(s_xn, 1)
            dve.wait_ge(s_gc, NC_)
            step(dve.transpose(gatesT, gates))
            dve.wait_ge(s_small, 16 * (2 * KD_ + 2))
            beta = t["beta"].rearrange("p (h m) -> p h m", h=H)
            for i in range(NH):
                step(dve.tensor_copy(beta[C * i:C * (i + 1), :, :],
                                     gt3[:, :, H * i:H * (i + 1)].rearrange("p m h -> p h m")))
            s3 = [soft[:, i, :].rearrange("p (h m) -> p h m", h=H) for i in range(5)]
            step(dve.tensor_tensor(s3[0], gt3[:, :, H * NH:].rearrange("p m h -> p h m"),
                                   dtb[:, :].unsqueeze(2).to_broadcast([C, H, P]), ALU.add))
            step(dve.tensor_scalar(soft[:, 1, :], soft[:, 0, :], -1.0, None, ALU.mult))
            dve.tensor_tensor(soft[:, 1, :], soft[:, 0, :], soft[:, 1, :], ALU.min).then_inc(s_gv, 1)
            dve.wait_ge(s_ga, 2)
            step(dve.tensor_scalar(soft[:, 3, :], soft[:, 2, :], 1.0, None, ALU.add))
            dve.tensor_scalar(soft[:, 4, :], soft[:, 3, :], -1.0, None, ALU.add).then_inc(s_gv, 1)
            dve.wait_ge(s_gv, 2)
            step(dve.tensor_tensor(soft[:, 4, :], soft[:, 2, :], soft[:, 4, :], ALU.subtract))
            dve.wait_ge(s_ga, 3)
            step(dve.reciprocal(soft[:, 2, :], soft[:, 3, :]))
            step(dve.tensor_tensor(soft[:, 4, :], soft[:, 4, :], soft[:, 2, :], ALU.mult))
            step(dve.tensor_tensor(soft[:, 4, :], soft[:, 4, :], soft[:, 1, :], ALU.add))
            step(dve.scalar_tensor_tensor(out=soft[:, 4, :], in0=soft[:, 0, :], scalar=0.0,
                                          in1=soft[:, 4, :], op0=ALU.max, op1=ALU.add))
            step(dve.tensor_scalar(expa[:, :], expa[:, :], -1.0, None, ALU.mult))
            step(dve.tensor_tensor(s3[4], s3[4], expa[:, :].unsqueeze(2).to_broadcast([C, H, P]),
                                   ALU.mult))
            dve.tensor_scalar(t["glog"][:, 0:n_gl], soft[:, 4, :], G_MIN, None, ALU.max).then_inc(s_gv, 1)
            dve.wait_ge(s_ga, 4)
            step(dve.tensor_scalar(t["beta"][:, :], t["beta"][:, :], 0.5, 0.5, ALU.mult, ALU.add))
            step(dve.reciprocal(t["beta"][:, :], t["beta"][:, :]))
            dve.wait_ge(s_eg, 2)
            step(dve.tensor_scalar(t["neg_eg"][:, :], t["neg_eg"][:, :], -1.0, None, ALU.mult))
            step(dve.memset(t["neg_eg"].rearrange("p (h m) -> p h m", h=H)[:, :, 0:B], 0.0))
            dve.wait_ge(s_lm, 1)
            for i in range(NH):
                step(dve.tensor_copy(t["lmask"][C * i:C * (i + 1), :, :], lm[:, :, :]))
                step(dve.tensor_copy(t["dmask"][C * i:C * (i + 1), :, :], dm[:, i, :, :]))
                step(dve.tensor_copy(t["mask0"][C * i:C * (i + 1), :], m0[:, i, :]))

        @block.scalar
        def _(act):
            def evac(m):
                act.wait_ge(s_tr, m + 1)
                k, j4 = m % 2, m // 2
                act.copy(xv[:, k, 0:NC_, 2 * j4:2 * j4 + 2, :].rearrange("p c b t -> p b c t"),
                         pt[:, m % 4, :].rearrange("p (b c t) -> p b c t", b=2, c=NC_)).then_inc(s_xt, 1)

            for q in range(QN):
                qs = slice(q * QT_, (q + 1) * QT_)
                act.wait_ge(s_cent, q + 1)
                act.activation(sq[:, :, :], xn[:, qs, :], ACT.Square).then_inc(s_sq, 1)
                act.wait_ge(s_var, q + 1)
                act.activation(stat[:, 2, qs], stat[:, 1, qs], ACT.Sqrt, bias=eps_ln[:, :],
                               scale=1.0 / D).then_inc(s_sd, 1)
                for m in range(q * QT_ // 2, (q + 1) * QT_ // 2):
                    evac(m)
            for c in range(NC_):
                act.wait_ge(s_g, c + 1)
                act.copy(gates[:, c * CB:(c + 1) * CB], pg[0:C, c % 2, :]).then_inc(s_gc, 1)
            act.wait_ge(s_small, 16 * (2 * KD_ + 2))
            act.activation(expa[:, :], alog[:, :], ACT.Exp).then_inc(s_ga, 1)
            act.wait_ge(s_gv, 1)
            act.activation(soft[:, 2, :], soft[:, 1, :], ACT.Exp).then_inc(s_ga, 1)
            act.wait_ge(s_ga, 2)
            act.activation(soft[:, 1, :], soft[:, 2, :], ACT.Ln, bias=one32[:, :]).then_inc(s_ga, 1)
            act.activation(t["beta"][:, :], t["beta"][:, :], ACT.Exp, scale=-1.0).then_inc(s_ga, 1)
            for m in range(2):
                act.wait_ge(s_g, NC_ + m + 1)
                act.activation(t["neg_eg"][:, m * 512:(m + 1) * 512], pg[0:R, m, :],
                               ACT.Exp).then_inc(s_eg, 1)

        @block.tensor
        def _(pe):
            for m in range(2 * NT // 4):
                k, j4 = m % 2, m // 2
                if m % (QT_ // 2) == 0:
                    pe.wait_ge(s_xn, m // (QT_ // 2) + 1)
                if m == 0:
                    pe.wait_ge(s_cst, 2)
                if m >= 4:
                    pe.wait_ge(s_xt, m - 3)
                for j in range(4):
                    last = pe.transpose(pt[:, m % 4, j * P:(j + 1) * P],
                                        xn[:, 4 * j4 + j, k * P:(k + 1) * P], ident[:, :])
                last.then_inc(s_tr, 1)
            pe.wait_ge(s_xt, 2 * NT // 4)
            pe.wait_ge(s_small, 16 * (2 * KD_ + 2))
            for c in range(NC_):
                if c >= 2:
                    pe.wait_ge(s_gc, c - 1)
                for k in range(KD_):
                    mm = pe.matmul(pg[0:C, c % 2, :], wab[:, k, :], t["xnT"][:, k, c, :],
                                   start=(k == 0), stop=(k == KD_ - 1))
                mm.then_inc(s_g, 1)
            pe.wait_ge(s_gv, 3)
            pe.wait_ge(s_gc, NC_)
            pe.wait_ge(s_lm, 1)
            for m in range(2):
                pe.matmul(pg[0:R, m, :], tri3[:, :], t["glog"][:, m * 512:(m + 1) * 512],
                          start=True, stop=True).then_inc(s_g, 1)


def attention(nc, t, ident, wq, wk, wv, wg, conv_q, conv_k, conv_v, o_dram, sem):
    with ExitStack() as ctx:
        def sb(name, shape, dt=F32):
            return ctx.enter_context(nc.sbuf_tensor(name, shape, dt))
        w_h = sb("w_h", [P, KD_, TT + 1, P])
        cw = sb("cw", [P, TT, CS])
        raw = sb("raw", [P, TT, B, C + CS - 1])
        cv = sb("cv", [P, TT, B, C])
        kq = sb("kq", [P, B, NH + 1, C])
        vq = sb("vq", [P, B, NH, C])
        ksq = sb("ksq", [P, B, NH, C])
        qsq = sb("qsq", [P, CB])
        gtri = sb("gtri", [C, B, C])
        ed = sb("ed", [R, B, C])
        egb = sb("egb", [P, B, C])
        dt_ = sb("dt_", [R, B, NH + 1, C])
        up = sb("up", [P, B, NH + 1, C])
        u0 = sb("u0", [R, B, R])
        zt = sb("zt", [R, B, R])
        yt = sb("yt", [R, B, R])
        p2 = sb("p2", [R, B, R // 2])
        p2l = sb("p2l", [R, B, R])
        state = sb("state", [P, B, HD])
        vs = sb("vs", [R, B, HD])
        kd = sb("kd", [R, B, HD])
        xs = sb("xs", [P, B, HD])
        gate_n = sb("gate_n", [P, CB])
        gate = sb("gate", [P, CB])
        osq = sb("osq", [P, CB])
        rt = sb("rt", [P, CB])
        og = sb("og", [P, CB])
        sm = sb("sm", [R, 6, B])
        sdec = sb("sdec", [P, B])
        tok = sb("tok", [C, 2, B])
        tok2 = sb("tok2", [C, B // 2, C])
        ps = lambda name, shape: ctx.enter_context(nc.psum_tensor(name, shape, F32))
        pj = ps("pj", [P, 2, 512])
        wa_ = ps("wa_", [P, 512])
        wb_ = ps("wb_", [P, 512])
        tb = ps("tb", [P, 2, 512])
        ta = ps("ta", [P, 2, 512])
        GW = [wa_, wb_]
        GT = [ta, tb]
        KKB = [wa_, wb_, tb[:, 0, :], tb[:, 1, :]]
        KSB = [tb[:, 0, :], tb[:, 1, :], ta[:, 0, :], ta[:, 1, :]]
        XB = [wa_, wb_, tb[:, 0, :], tb[:, 1, :]]
        SUB = [ta[:, 1, :], wa_, wb_, tb[:, 0, :]]
        o_ps, rms_ps, n_ps = ta[:, 0, :], tb[:, 1, :], ta[:, 1, :]

        S = {n: sem("m_" + n) for n in (
            "w", "item", "item_out", "norm", "kkp", "z0t", "qs", "tok", "p2", "zn", "ytt", "ks", "x",
            "o", "su", "rms", "small", "up", "y0", "p2m", "zadd", "r", "state", "halo", "conv", "rr",
            "t1", "sn", "z0", "y", "xo", "silu", "osq", "rt", "gtri", "dt", "ksq", "qsq",
            "gate", "u0", "yi", "og", "stored", "passed")}
        W_DMAS = 2 * 8 + 3
        NSM = 7
        NCV = (CS - 1) * TT
        NTOK = 4

        def lo_hi(ap3, lev, half):
            w = 1 << lev
            return ap3.rearrange("p b (m two w) -> p b m two w", two=2, w=w)[:, :, :, half, :]

        block = ctx.enter_context(nc.Block())

        @block.sync
        def _(sp):
            def load_head(h):
                for k in range(KD_):
                    rowsl = slice(k * P, (k + 1) * P)
                    for src, t0, n in ((wk, 0, NH), (wv, NH + 1, NH)):
                        v = src[rowsl, :].rearrange("p (i h c) -> p i h c", i=NH, h=H)
                        for i in range(NH):
                            sp.dma_start(w_h[:, k, t0 + i, :], v[:, i, bass.ds(h, 1), :].rearrange(
                                "p a c -> p (a c)")).then_inc(S["w"], 16)
                    for src, t0 in ((wq, QT), (wg, GATE)):
                        v = src[rowsl, :].rearrange("p (h c) -> p h c", h=H)
                        sp.dma_start(w_h[:, k, t0, :], v[:, bass.ds(h, 1), :].rearrange(
                            "p a c -> p (a c)")).then_inc(S["w"], 16)
                for src, t0, n in ((conv_k, 0, NH), (conv_q, QT, 1), (conv_v, NH + 1, NH)):
                    v = src.rearrange("(i h p) w -> p i h w", i=n, h=H)
                    sp.dma_start(cw[:, t0:t0 + n, :], v[:, :, bass.ds(h, 1), :].rearrange(
                        "p i a w -> p i (a w)"), allow_slow_non_contiguous=True).then_inc(S["w"], 16)

            def store(h, c, it):
                sp.wait_ge(S["og"], it + 1)
                sp.dma_start(o_dram[bass.ds(h, 1), :, :, bass.ds(c * C, C)].rearrange("a p b t -> (a p) b t"),
                             og[:, :].rearrange("p (b t) -> p b t", b=B)).then_inc(S["stored"], 16)

            sp.sem_inc(S["stored"], 16)
            load_head(0)
            with sp.Fori(0, H - 1) as h:
                with sp.Fori(0, NC_ - 1) as c:
                    store(h, c, h * NC_ + c)
                load_head(h + 1)
                store(h, NC_ - 1, h * NC_ + NC_ - 1)
            with sp.Fori(0, NC_ - 1) as c:
                store(H - 1, c, (H - 1) * NC_ + c)
            load_head(0)
            store(H - 1, NC_ - 1, IT - 1)
            sp.wait_ge(S["stored"], 16 * (IT + 1))
            sp.wait_ge(S["w"], 16 * W_DMAS * (H + 1))

        @block.tensor
        def _(pe):
            def item(kind, a, base, k, it, chunk):
                bank = pj[:, k % 2, :]
                if not (it is None and k < 2):
                    pe.wait_ge(S["item_out"], base + k - 1)
                if kind == "d":
                    pe.wait_ge(S["gtri"], 1 if it is None else it + 2)
                    mm = pe.matmul(bank[0:R, :], t["suf3"][:, :], gtri[:, :, :], start=True, stop=True)
                elif kind == "e":
                    mm = pe.matmul(bank, t["ones"][0:C, :], gtri[:, :, :], start=True, stop=True)
                elif kind in "cg":
                    tile = a if kind == "c" else GATE
                    for h2 in range(KD_):
                        mm = pe.matmul(bank, w_h[:, h2, tile, :], chunk(h2),
                                       start=(h2 == 0), stop=(h2 == KD_ - 1))
                else:
                    src = kq if kind == "kn" else vq
                    for j in range(4):
                        mm = pe.transpose(bank[0:R, j * HD:(j + 1) * HD],
                                          src[:, 4 * a + j, 0:NH, :], ident[:, :])
                mm.then_inc(S["item"], 1)

            pe.wait_ge(S["w"], 16 * W_DMAS)
            for k, (kind, a) in enumerate(FIRST):
                item(kind, a, 0, k, None, lambda h2: t["xnT"][:, h2, 0, :])

            with pe.Fori(0, IT) as it:
                base = it * NS + N0
                nxt = (it + 1) % NC_

                def chunk(h2):
                    return t["xnT"][:, h2, bass.ds(nxt, 1), :].rearrange("p a c -> p (a c)")

                todo = [(k, *s) for k, s in enumerate(STREAM)]

                def stream(n):
                    for _ in range(n):
                        k, kind, a = todo.pop(0)
                        if kind == "c" and a == 0:
                            pe.wait_ge(S["w"], wneed)
                        item(kind, a, base, k, it, chunk)

                wneed = ((it + 1) // NC_ + 1) * (16 * W_DMAS)
                pe.wait_ge(S["ksq"], it + 1)
                pe.wait_ge(S["state"], it * 4 + 1)
                for b in range(B):
                    mm = pe.matmul(n_ps[0:R, b:b + 1], ksq[:, b, :, :], t["ones"][:, 0:1],
                                   start=True, stop=True)
                mm.then_inc(S["norm"], 1)
                pe.wait_ge(S["silu"], (it + 1) * TT)
                for g in range(4):
                    if g == 3:
                        pe.wait_ge(S["sn"], it + 1)
                    for j in range(4):
                        b = 4 * g + j
                        mm = pe.matmul(KKB[g][0:R, j * P:(j + 1) * P], kq[:, b, 0:NH, :],
                                       kq[:, b, :, :], start=True, stop=True)
                    mm.then_inc(S["kkp"], 1)
                stream(6)
                for g in range(2):
                    if g == 1:
                        stream(1)
                    pe.wait_ge(S["y0"], 2 * it + g + 1)
                    for j in range(8):
                        mm = pe.transpose(GT[g][0:R, j // 4, (j % 4) * P:(j % 4) * P + R],
                                          yt[:, 8 * g + j, :], ident[0:R, 0:R])
                    mm.then_inc(S["z0t"], 1)
                stream(2)
                for lev in range(LEVELS):
                    last = lev == LEVELS - 1
                    for g in range(2):
                        if lev == 0:
                            pe.wait_ge(S["z0"], 2 * it + g + 1)
                        else:
                            pe.wait_ge(S["zadd"], 2 * LEVELS * it + 2 * lev + g - 1)
                        for j in range(8):
                            b = 8 * g + j
                            mm = pe.matmul(GW[g][0:R, j * R // 2:(j + 1) * R // 2], up[0:R, b, 0:NH, :],
                                           lo_hi(zt, lev, 0)[:, b], start=True, stop=True)
                        mm.then_inc(S["p2"], 1)
                    stream(N_AFTER[lev][0])
                    for g in range(2):
                        pe.wait_ge(S["p2m"], 2 * LEVELS * it + 2 * lev + g + 1)
                        if lev > 0:
                            pe.wait_ge(S["y"], 2 * (LEVELS - 1) * it + 2 * lev + g - 1)
                        for j in range(8):
                            b = 8 * g + j
                            if last:
                                lhs, rhs = p2l[:, b, :], lo_hi(yt, lev, 1)[:, b]
                            else:
                                lhs, rhs = yt[:, b, :], p2[:, b, :]
                            mm = pe.matmul(GW[g][0:R, j * R // 2:(j + 1) * R // 2], lhs, rhs,
                                           start=True, stop=True)
                        mm.then_inc(S["zn"], 1)
                    stream(N_AFTER[lev][1])
                    if not last:
                        for g in range(2):
                            pe.wait_ge(S["zadd"], 2 * LEVELS * it + 2 * lev + g + 1)
                            for j in range(8):
                                mm = pe.transpose(GT[g][0:R, j // 4, (j % 4) * P:(j % 4) * P + R],
                                                  zt[:, 8 * g + j, :], ident[0:R, 0:R])
                            mm.then_inc(S["ytt"], 1)
                assert not todo
                for g in range(4):
                    for j in range(4):
                        b = 4 * g + j
                        mm = pe.matmul(KSB[g][:, j * HD:(j + 1) * HD], kq[:, b, :, :],
                                       state[:, b, :], start=True, stop=True)
                    mm.then_inc(S["ks"], 1)
                for g in range(4):
                    if g % 2 == 0:
                        pe.wait_ge(S["zadd"], 2 * LEVELS * it + 2 * LEVELS - 1 + g // 2)
                    pe.wait_ge(S["r"], 4 * it + g + 1)
                    if g >= 2:
                        pe.wait_ge(S["qs"], 4 * it + g - 1)
                    if g == 0:
                        pe.wait_ge(S["zadd"], 2 * LEVELS * (it + 1))
                    for j in range(4):
                        b = 4 * g + j
                        mm = pe.matmul(XB[g][0:R, j * HD:(j + 1) * HD], yt[:, b, :], vs[:, b, :],
                                       start=True, stop=True)
                    mm.then_inc(S["x"], 1)
                pe.wait_ge(S["qs"], 4 * (it + 1))
                pe.wait_ge(S["small"], NSM * (it + 1))
                for g in range(4):
                    pe.wait_ge(S["xo"], 4 * it + g + 1)
                    for j in range(4):
                        b = 4 * g + j
                        mm = pe.matmul(o_ps[:, b * C:(b + 1) * C], xs[:, b, :], up[:, b, NH, :],
                                       start=True, stop=True)
                mm.then_inc(S["o"], 1)
                for g in range(4):
                    for j in range(4):
                        b = 4 * g + j
                        mm = pe.matmul(SUB[g][:, j * HD:(j + 1) * HD], kd[:, b, :], xs[0:R, b, :],
                                       start=True, stop=True)
                    mm.then_inc(S["su"], 1)
                pe.wait_ge(S["osq"], it + 1)
                pe.matmul(rms_ps, t["one_d"][:, :], osq[:, :], start=True, stop=False)
                pe.matmul(rms_ps, t["eps_d"][:, :], qsq[:, :], start=False, stop=True).then_inc(S["rms"], 1)

        @block.scalar
        def _(act):
            def item(kind, a, base, k, it):
                bank = pj[:, k % 2, :]
                nxt = 0 if it is None else it + 1
                act.wait_ge(S["item"], base + k + 1)
                if kind == "d":
                    if it is not None:
                        act.wait_ge(S["dt"], it + 1)
                        act.wait_ge(S["small"], NSM * (it + 1))
                    ins = act.activation(ed[:, :, :], bank[0:R, :], ACT.Exp)
                elif kind == "e":
                    if it is not None:
                        act.wait_ge(S["small"], NSM * (it + 1))
                    bias = t["start"][:, 0:1] if it is None else t["start"][:, bass.ds(nxt, 1)]
                    ins = act.activation(egb[:, :, :], bank, ACT.Exp, bias=bias)
                elif kind == "c":
                    if a == 0:
                        act.wait_ge(S["halo"], 1 if it is None else it + 2)
                    act.copy(raw[:, a, :, CS - 1:], bank)
                    ins = act.mul(cv[:, a, :, :], bank, cw[:, a, CS - 1:CS])
                elif kind == "g":
                    if it is not None:
                        act.wait_ge(S["gate"], it + 1)
                    ins = act.activation(gate_n[:, :], bank, ACT.Silu)
                elif kind == "kn":
                    if a == 0:
                        act.wait_ge(S["small"], NSM * it + 4)
                    for j in range(4):
                        b = 4 * a + j
                        ins = act.mul(kd[:, b, :], bank[0:R, j * HD:(j + 1) * HD], sm[:, 3, b:b + 1])
                else:
                    for j in range(4):
                        b = 4 * a + j
                        ins = act.mul(vs[:, b, :], bank[0:R, j * HD:(j + 1) * HD], sm[:, 4, b:b + 1])
                ins.then_inc(S["item_out"], 1)

            def silu(tile, it):
                nxt = 0 if it is None else it + 1
                act.wait_ge(S["conv"], nxt * NCV + (CS - 1) * (tile + 1))
                dst = kq[:, :, tile, :] if tile <= QT else vq[:, :, tile - QT - 1, :]
                act.activation(dst, cv[:, tile, :, :], ACT.Silu).then_inc(S["silu"], 1)

            for k, (kind, a) in enumerate(FIRST):
                item(kind, a, 0, k, None)
            for tile in range(TT):
                silu(tile, None)

            with act.Fori(0, IT) as it:
                base = it * NS + N0
                todo = [(k, *s) for k, s in enumerate(STREAM)]

                def stream(n):
                    for _ in range(n):
                        k, kind, a = todo.pop(0)
                        item(kind, a, base, k, it)

                act.wait_ge(S["small"], NSM * it + 1)
                act.activation(sm[:, 4, :], sm[:, 0, :], ACT.Sqrt).then_inc(S["sn"], 1)
                act.wait_ge(S["sn"], it + 1)
                stream(6)
                for g in range(2):
                    if g == 1:
                        stream(1)
                    act.wait_ge(S["z0t"], 2 * it + g + 1)
                    act.copy(zt[:, 8 * g:8 * g + 8, :],
                             GT[g][0:R, :, :].rearrange("p k (j r) -> p (k j) r", r=P)[:, :, 0:R]
                             ).then_inc(S["z0"], 1)
                stream(2)
                for lev in range(LEVELS):
                    stream(N_AFTER[lev][0])
                    stream(N_AFTER[lev][1])
                    if lev < LEVELS - 1:
                        w = 1 << lev
                        for g in range(2):
                            act.wait_ge(S["ytt"], 2 * (LEVELS - 1) * it + 2 * lev + g + 1)
                            src = GT[g][0:R, :, :].rearrange("p k (j m two w) -> p (k j) m two w",
                                                            two=2, w=w, m=P // (2 * w))
                            act.copy(lo_hi(yt, lev, 1)[:, 8 * g:8 * g + 8],
                                     src[:, :, 0:R // (2 * w), 1, :]).then_inc(S["y"], 1)
                for g in range(4):
                    act.wait_ge(S["ks"], 4 * it + g + 1)
                    act.copy(xs[R:, 4 * g:4 * g + 4, :], KSB[g][R:, :]).then_inc(S["qs"], 1)
                for g in range(4):
                    act.wait_ge(S["x"], 4 * it + g + 1)
                    act.copy(xs[0:R, 4 * g:4 * g + 4, :], XB[g][0:R, :]).then_inc(S["xo"], 1)
                act.wait_ge(S["qsq"], it + 1)
                for tile in range(NH):
                    silu(tile, it)
                act.wait_ge(S["o"], it + 1)
                act.activation(osq[:, :], o_ps, ACT.Square).then_inc(S["osq"], 1)
                for tile in range(NH, TT):
                    silu(tile, it)
                act.wait_ge(S["rms"], it + 1)
                act.activation(rt[:, :], rms_ps, ACT.Sqrt, bias=t["eps_rms"][:, :]).then_inc(S["rt"], 1)

        @block.vector
        def _(dve):
            def halo(keep, n):
                dve.tensor_scalar(raw[:, :, :, 0:CS - 1].rearrange("p t b w -> p (t b) w"),
                                  raw[:, :, :, C:].rearrange("p t b w -> p (t b) w"),
                                  keep, None, ALU.mult).then_inc(S["halo"], 1)

            def conv(tile, it):
                base = 0 if it is None else it * NS + N0
                k = (FIRST if it is None else STREAM).index(("c", tile))
                nxt = 0 if it is None else it + 1
                dve.wait_ge(S["item_out"], base + k + 1)
                for i in range(CS - 2, -1, -1):
                    n = nxt * NCV + (CS - 1) * tile + (CS - 2 - i)
                    if i < CS - 2:
                        dve.wait_ge(S["conv"], n)
                    dve.scalar_tensor_tensor(out=cv[:, tile, :, :], in0=raw[:, tile, :, i:i + C],
                                             scalar=cw[:, tile, i:i + 1], in1=cv[:, tile, :, :],
                                             op0=ALU.mult, op1=ALU.add).then_inc(S["conv"], 1)

            dve.memset(p2l[:, :, :], 0.0)
            dve.memset(state[:, :, :], 0.0).then_inc(S["state"], 1)
            dve.memset(raw[:, :, :, 0:CS - 1], 0.0).then_inc(S["halo"], 1)
            dve.wait_ge(S["w"], 16 * W_DMAS)
            for tile in range(TT):
                conv(tile, None)

            with dve.Fori(0, IT) as it:
                base = it * NSM
                cols = bass.ds(it * B, B)
                dve.wait_ge(S["norm"], it + 1)
                dve.tensor_scalar(sm[:, 0, :], n_ps[0:R, 0:B], L2_EPS, None, ALU.add).then_inc(S["small"], 1)
                dve.wait_ge(S["small"], base + 1)
                dve.reciprocal(sm[:, 1, :], sm[:, 0, :]).then_inc(S["small"], 1)
                dve.wait_ge(S["small"], base + 2)
                dve.tensor_tensor(sm[:, 2, :], sm[:, 1, :], t["beta"][:, cols], ALU.mult).then_inc(S["small"], 1)
                dve.wait_ge(S["small"], base + 3)
                dve.tensor_tensor(sm[:, 3, :], sm[:, 2, :], ed[:, :, C - 1], ALU.mult).then_inc(S["small"], 1)
                dve.tensor_copy(sm[:, 5, :], t["neg_eg"][:, cols]).then_inc(S["small"], 1)
                dve.tensor_copy(sdec[:, :], egb[:, :, C - 1]).then_inc(S["small"], 1)
                dve.tensor_tensor(up[R:, :, NH, :], egb[R:, :, :],
                                  ident[R:, R:].unsqueeze(1).to_broadcast([C, B, C]),
                                  ALU.mult).then_inc(S["small"], 1)
                dve.wait_ge(S["dt"], it + 1)
                for g in range(4):
                    dve.wait_ge(S["kkp"], 4 * it + g + 1)
                    for j in range(4):
                        b = 4 * g + j
                        ins = dve.scalar_tensor_tensor(
                            out=up[0:R, b, :, :], in0=KKB[g][0:R, j * P:(j + 1) * P].rearrange(
                                "p (i c) -> p i c", c=C),
                            scalar=sm[:, 2, b:b + 1], in1=dt_[:, b, :, :], op0=ALU.mult, op1=ALU.mult)
                    ins.then_inc(S["up"], 1)
                halo(t["keep"][:, bass.ds(it + 1, 1)], it)
                for g in range(2):
                    bs = slice(8 * g, 8 * g + 8)
                    nt = NTOK * (2 * it + g)
                    dve.wait_ge(S["u0"], 2 * it + g + 1)
                    dve.tensor_reduce(tok[:, 0, bs], u0[0:C, bs, C:2 * C], AX_X, ALU.add).then_inc(S["tok"], 1)
                    dve.tensor_reduce(tok[:, 1, bs], u0[C:2 * C, bs, 2 * C:], AX_X, ALU.add
                                      ).then_inc(S["tok"], 1)
                    dve.wait_ge(S["tok"], nt + 2)
                    dve.tensor_tensor(tok[:, 0, bs], tok[:, 0, bs], tok[:, 1, bs], ALU.mult
                                      ).then_inc(S["tok"], 1)
                    dve.wait_ge(S["tok"], nt + 3)
                    dve.tensor_tensor(tok2[:, :, :], tok[:, 0, bs].unsqueeze(2).to_broadcast([C, 8, C]),
                                      ident[0:C, 0:C].unsqueeze(1).to_broadcast([C, 8, C]), ALU.mult
                                      ).then_inc(S["tok"], 1)
                    dve.wait_ge(S["tok"], nt + 4)
                    dve.wait_ge(S["yi"], 2 * it + g + 1)
                    dve.tensor_tensor(yt[0:C, bs, 2 * C:], yt[0:C, bs, 2 * C:], tok2[:, :, :],
                                      ALU.add).then_inc(S["y0"], 1)
                conv(0, it)
                conv(1, it)
                for lev in range(LEVELS):
                    last = lev == LEVELS - 1
                    for g in range(2):
                        n = 2 * LEVELS * it + 2 * lev + g + 1
                        dve.wait_ge(S["p2"], n)
                        src = GW[g][0:R, 0:4 * R].rearrange("p (j c) -> p j c", j=8)
                        mask = t["lmask"][:, lev, :].unsqueeze(1).to_broadcast([R, 8, R // 2])
                        if last:
                            w = C // 2
                            dve.tensor_tensor(
                                lo_hi(p2l, lev, 0)[:, 8 * g:8 * g + 8],
                                src.rearrange("p j (m w) -> p j m w", w=w),
                                mask.rearrange("p j (m w) -> p j m w", w=w), ALU.mult).then_inc(S["p2m"], 1)
                        else:
                            dve.tensor_tensor(p2[:, 8 * g:8 * g + 8, :], src, mask,
                                              ALU.mult).then_inc(S["p2m"], 1)
                    if lev == 0:
                        conv(2, it)
                    for g in range(2):
                        n = 2 * LEVELS * it + 2 * lev + g + 1
                        dve.wait_ge(S["zn"], n)
                        w = 1 << lev
                        dst = lo_hi(yt, lev, 1) if last else lo_hi(zt, lev, 0)
                        dst = dst[:, 8 * g:8 * g + 8]
                        dve.tensor_tensor(
                            dst, GW[g][0:R, 0:4 * R].rearrange("p (j m w) -> p j m w", j=8, w=w), dst,
                            ALU.add).then_inc(S["zadd"], 1)
                    if lev < 4:
                        conv(lev + 3, it)
                for g in range(4):
                    dve.wait_ge(S["ks"], 4 * it + g + 1)
                    if g == 0:
                        dve.wait_ge(S["item_out"], it * NS + N0 + NS - 2)
                    for j in range(4):
                        b = 4 * g + j
                        ins = dve.scalar_tensor_tensor(
                            out=vs[:, b, :], in0=KSB[g][0:R, j * HD:(j + 1) * HD],
                            scalar=sm[:, 5, b:b + 1], in1=vs[:, b, :], op0=ALU.mult, op1=ALU.add)
                    ins.then_inc(S["r"], 1)
                for g in range(4):
                    dve.wait_ge(S["su"], 4 * it + g + 1)
                    for j in range(4):
                        b = 4 * g + j
                        ins = dve.scalar_tensor_tensor(
                            out=state[:, b, :], in0=state[:, b, :], scalar=sdec[:, b:b + 1],
                            in1=SUB[g][:, j * HD:(j + 1) * HD], op0=ALU.mult, op1=ALU.add)
                    ins.then_inc(S["state"], 1)
                dve.wait_ge(S["rt"], it + 1)
                dve.reciprocal(rt[:, :], rt[:, :]).then_inc(S["rr"], 1)
                dve.wait_ge(S["rr"], it + 1)
                dve.tensor_tensor(rt[:, :], o_ps, rt[:, :], ALU.mult).then_inc(S["t1"], 1)

        @block.gpsimd
        def _(pool):
            def make_gtri(it):
                g = t["glog"][:, 0:B] if it is None else t["glog"][:, bass.ds((it + 1) * B, B)]
                pool.tensor_tensor(gtri[:, :, :], g.unsqueeze(2).to_broadcast([C, B, C]),
                                   t["tri"][:, :].unsqueeze(1).to_broadcast([C, B, C]),
                                   ALU.mult).then_inc(S["gtri"], 1)

            def make_dt(base, it):
                k = (FIRST if it is None else STREAM).index(("d", 0))
                pool.wait_ge(S["item_out"], base + k + 1)
                if it is not None:
                    pool.wait_ge(S["up"], 4 * (it + 1))
                pool.tensor_tensor(dt_[:, :, :, :], ed[:, :, :].unsqueeze(2).to_broadcast([R, B, NH + 1, C]),
                                   t["dmask"][:, :, :].unsqueeze(1).to_broadcast([R, B, NH + 1, C]),
                                   ALU.mult).then_inc(S["dt"], 1)

            def make_ksq(nxt):
                pool.wait_ge(S["silu"], nxt * TT + NH)
                pool.tensor_tensor(ksq[:, :, :, :], kq[:, :, 0:NH, :], kq[:, :, 0:NH, :],
                                   ALU.mult).then_inc(S["ksq"], 1)

            make_gtri(None)
            make_dt(0, None)
            make_ksq(0)
            with pool.Fori(0, IT) as it:
                base = it * NS + N0
                pool.wait_ge(S["silu"], (it + 1) * TT)
                pool.wait_ge(S["norm"], it + 1)
                pool.tensor_tensor(qsq[:, :].rearrange("p (b c) -> p b c", c=C), kq[:, :, QT, :], kq[:, :, QT, :],
                                   ALU.mult).then_inc(S["qsq"], 1)
                make_gtri(it)
                for g in range(2):
                    bs = slice(8 * g, 8 * g + 8)
                    pool.wait_ge(S["up"], 4 * it + 2 * g + 2)
                    pool.tensor_tensor(u0[:, bs, :], up[0:R, bs, 0:NH, :].rearrange("p b i c -> p b (i c)"),
                                       t["mask0"][:, :].unsqueeze(1).to_broadcast([R, 8, R]),
                                       ALU.mult).then_inc(S["u0"], 1)
                pool.wait_ge(S["stored"], 16 * (it + 1))
                pool.sem_inc(S["passed"], 1)
                pool.tensor_copy(gate[:, :], gate_n[:, :]).then_inc(S["gate"], 1)
                for g in range(2):
                    bs = slice(8 * g, 8 * g + 8)
                    pool.wait_ge(S["u0"], 2 * it + g + 1)
                    pool.tensor_tensor(yt[:, bs, :], u0[:, bs, :],
                                       ident[0:R, 0:R].unsqueeze(1).to_broadcast([R, 8, R]),
                                       ALU.add).then_inc(S["yi"], 1)
                make_dt(base, it)
                make_ksq(it + 1)
                pool.wait_ge(S["t1"], it + 1)
                pool.tensor_tensor(og[:, :], rt[:, :], gate[:, :], ALU.mult).then_inc(S["og"], 1)


def project_and_route(nc, k, ident, wo, rms_weight, router_w, h_dram, o_dram, xe_dram, sem):
    G = 4
    NG = NT // G
    GT_ = G * P
    with ExitStack() as ctx:
        def sb(name, shape, dt=F32):
            return ctx.enter_context(nc.sbuf_tensor(name, shape, dt))
        wo_s = sb("wo_s", [P, H, D])
        rw = sb("rw", [P, 1])
        rt_w = sb("rt_w", [P, KD_, E])
        o_in = sb("o_in", [P, 2, H, GT_])
        h_in = sb("h_in", [P, 2, G, D])
        hs = sb("hs", [P, G, D])
        xc = sb("xc", [P, 2, G, D])
        sq = sb("c_sq", [P, G, D])
        xT = sb("xT", [P, KD_, GT_])
        st = sb("st", [P, 5, G])
        eps = sb("c_eps", [P, 1])
        lg = sb("lg", [P, G, E])
        ex = sb("ex", [P, G, E])
        oh = sb("oh", [P, G, E])
        ohb = sb("ohb", [P, G, E], BF16)
        tmp = sb("tmp", [P, G, E])
        sc = sb("sc", [P, 8, G])
        slot = sb("slot", [P, 2, G], I32)
        carry = sb("carry", [P, E])
        rank = sb("rank", [P, E])
        ebase = sb("ebase", [P, E])
        trash = sb("trash", [P, NT])
        trif = sb("trif", [P, P])
        onesf = sb("onesf", [P, P])
        trib = sb("trib", [P, P], BF16)
        onesb = sb("onesb", [P, P], BF16)
        pr = [ctx.enter_context(nc.psum_tensor(f"pr{u}", [P, G, D], F32)) for u in range(2)]
        tp = ctx.enter_context(nc.psum_tensor("tp", [P, KD_, 512], F32))
        lp = ctx.enter_context(nc.psum_tensor("lp", [P, 512], F32))
        cp = ctx.enter_context(nc.psum_tensor("cp", [P, 512], F32))

        s_w, s_rw = sem("c_w"), sem("c_rw")
        s_in = [sem(f"c_in{u}") for u in range(2)]
        s_scat, s_sent, s_passed = sem("c_scat"), sem("c_sent"), sem("c_passed")
        s_c, s_ws, s_pr, s_hs, s_keep, s_v = (sem("c_" + n) for n in ("c", "ws", "pr", "hs", "keep", "v"))
        s_cen, s_sq, s_var, s_sd, s_xn, s_tr, s_xt = (
            sem("c_" + n) for n in ("cen", "sqr", "var", "sd", "xn", "tr", "xt"))
        s_lg, s_ls, s_ex, s_oh, s_pos, s_slot = (
            sem("c_" + n) for n in ("lg", "ls", "ex", "oh", "pos", "slot"))
        h_v = h_dram.rearrange("(g j p) d -> g p j d", j=G, p=P)
        block = ctx.enter_context(nc.Block())

        def groups(eng, body):
            with eng.Fori(0, NG // 2 - 1) as i:
                for u in range(2):
                    body(i * 2 + u, u, True)
            for u in range(2):
                body(NG - 2 + u, u, u == 0)

        @block.sync
        def _(sp):
            sp.dma_start(wo_s[:, :, :], wo.rearrange("(h p) n -> p h n", h=H)).then_inc(s_w, 16)
            sp.dma_start(rw[:, :], rms_weight.unsqueeze(1)).then_inc(s_w, 16)

            def load(g, u):
                for hh in range(H):
                    src = o_dram[hh].rearrange("p (g b) t -> p g (b t)", b=GT_ // T)
                    sp.dma_start(o_in[:, u, hh, :], src[:, bass.ds(g, 1), :].rearrange(
                        "p a c -> p (a c)")).then_inc(s_in[u], 16)
                sp.dma_start(h_in[:, u, :, :], h_v[bass.ds(g, 1)].rearrange(
                    "a p j d -> (a p) j d")).then_inc(s_in[u], 16)

            load(0, 0)
            load(1, 1)
            for kk in range(KD_):
                sp.dma_start(rt_w[:, kk, :], router_w[:, kk * P:(kk + 1) * P].rearrange("e p -> p e"),
                             allow_slow_non_contiguous=True).then_inc(s_rw, 16)
            with sp.Fori(0, NG // 2 - 1) as i:
                for u in range(2):
                    sp.wait_ge(s_hs, i * 2 + (u + 3))
                    load(i * 2 + (u + 2), u)

        @block.gpsimd
        def _(pool):
            n = [0]

            def step(ins):
                n[0] += 1
                ins.then_inc(s_c, 1)
                pool.wait_ge(s_c, n[0])

            step(pool.memset(trif[:, :], 1.0))
            step(pool.affine_select(out=trif[:, :], in_=trif[:, :], compare_op=ALU.is_ge, fill=0.0, base=0,
                                    pattern=[[1, P]], channel_multiplier=-1))
            step(pool.iota(rank[:, :], [[-1, E]], base=E, channel_multiplier=0,
                           allow_small_or_imprecise_dtypes=True))
            step(pool.iota(ebase[:, :], [[CAP, E]], base=0, channel_multiplier=0,
                           allow_small_or_imprecise_dtypes=True))
            step(pool.iota(trash[:, :], [[P, NT]], base=TRASH, channel_multiplier=1,
                           allow_small_or_imprecise_dtypes=True))

            def body(g, u, more):
                pool.wait_ge(s_hs, g + 3)
                pool.sem_inc(s_passed, 1)
                pool.tensor_copy(k["h2"][:, bass.ds(g * G, G), :], hs[:, :, :]).then_inc(s_keep, 1)
                pool.wait_ge(s_slot, g + 1)
                pool.sem_inc(s_passed, 1)
                for j in range(G):
                    pool.indirect_dma_start(xe_dram, bass.IndirectOffsetOnAxis(ap=slot[:, u, j:j + 1], axis=0),
                                            xc[:, u, j, :], None).then_inc(s_scat, 16)
                pool.wait_ge(s_scat, g * (16 * G) + 16 * G)
                pool.sem_inc(s_sent, 1)

            groups(pool, body)

        @block.tensor
        def _(pe):
            def project(g, u):
                pe.wait_ge(s_in[u], GROUP_IN * (g // 2 + 1))
                pe.wait_ge(s_hs, g + 1)
                for j in range(G):
                    for hh in range(H):
                        mm = pe.matmul(pr[u][:, j, :], o_in[:, u, hh, j * P:(j + 1) * P], wo_s[:, hh, :],
                                       start=(hh == 0), stop=(hh == H - 1))
                mm.then_inc(s_pr, 1)

            GROUP_IN = 16 * (H + 1)
            pe.wait_ge(s_ws, 2)
            project(0, 0)
            pe.wait_ge(s_rw, 16 * KD_)
            pe.wait_ge(s_v, 2)

            def body(g, u, more):
                if more:
                    project(g + 1, 1 - u)
                pe.wait_ge(s_xn, g + 1)
                for kk in range(KD_):
                    for j in range(G):
                        mm = pe.transpose(tp[:, kk, j * P:(j + 1) * P], xc[:, u, j, kk * P:(kk + 1) * P],
                                          ident[:, :])
                mm.then_inc(s_tr, 1)
                pe.wait_ge(s_xt, g + 1)
                for j in range(G):
                    for kk in range(KD_):
                        mm = pe.matmul(lp[:, j * E:(j + 1) * E], xT[:, kk, j * P:(j + 1) * P], rt_w[:, kk, :],
                                       start=(kk == 0), stop=(kk == KD_ - 1))
                mm.then_inc(s_lg, 1)
                pe.wait_ge(s_oh, g + 1)
                for j in range(G):
                    for i in range(j + 1):
                        pe.matmul(cp[:, j * E:(j + 1) * E], (trib if i == j else onesb)[:, :], ohb[:, i, :],
                                  start=(i == 0), stop=(i == j))
                for i in range(G):
                    mm = pe.matmul(cp[:, G * E:(G + 1) * E], onesb[:, :], ohb[:, i, :],
                                   start=(i == 0), stop=(i == G - 1))
                mm.then_inc(s_pos, 1)

            groups(pe, body)

        @block.scalar
        def _(act):
            act.wait_ge(s_w, 32)
            for hh in range(H):
                ins = act.mul(wo_s[:, hh, :], wo_s[:, hh, :], rw[:, 0:1])
            ins.then_inc(s_ws, 1)
            act.wait_ge(s_ws, 2)

            def body(g, u, more):
                act.wait_ge(s_cen, g + 1)
                act.activation(sq[:, :, :], xc[:, u, :, :], ACT.Square).then_inc(s_sq, 1)
                act.wait_ge(s_var, g + 1)
                act.activation(st[:, 2, :], st[:, 1, :], ACT.Sqrt, bias=eps[:, :],
                               scale=1.0 / D).then_inc(s_sd, 1)
                act.wait_ge(s_tr, g + 1)
                act.copy(xT[:, :, :], tp[:, :, :]).then_inc(s_xt, 1)
                act.wait_ge(s_ls, g + 1)
                act.activation(ex[:, :, :], lg[:, :, :], ACT.Exp).then_inc(s_ex, 1)

            groups(act, body)

        @block.vector
        def _(dve):
            dve.sem_inc(s_hs, 2)
            dve.sem_inc(s_keep, 1)
            dve.sem_inc(s_sent, 2)
            dve.memset(eps[:, :], LN_EPS)
            dve.memset(onesf[:, :], 1.0)
            dve.memset(carry[:, :], 0.0)
            dve.drain().then_inc(s_ws, 1)
            dve.wait_ge(s_c, 5)
            dve.wait_ge(s_ws, 1)
            dve.tensor_copy(onesb[:, :], onesf[:, :]).then_inc(s_v, 1)
            dve.tensor_copy(trib[:, :], trif[:, :]).then_inc(s_v, 1)

            def bc(a, n):
                return a.unsqueeze(2).to_broadcast([P, G, n])

            NV = 21

            def body(g, u, more):
                m = [0]

                def step(ins):
                    m[0] += 1
                    ins.then_inc(s_v, 1)
                    dve.wait_ge(s_v, g * NV + (2 + m[0]))

                dve.wait_ge(s_pr, g + 1)
                dve.wait_ge(s_keep, g + 1)
                dve.wait_ge(s_in[u], 16 * (H + 1) * (g // 2 + 1))
                dve.tensor_tensor(hs[:, :, :], pr[u][:, :, :], h_in[:, u, :, :], ALU.add).then_inc(s_hs, 1)
                dve.wait_ge(s_hs, g + 3)
                step(dve.tensor_reduce(st[:, 0, :], hs[:, :, :], AX_X, ALU.add))
                step(dve.tensor_scalar(st[:, 0, :], st[:, 0, :], -1.0 / D, None, ALU.mult))
                dve.wait_ge(s_sent, g + 1)
                dve.tensor_tensor(xc[:, u, :, :], hs[:, :, :], bc(st[:, 0, :], D), ALU.add).then_inc(s_cen, 1)
                dve.wait_ge(s_sq, g + 1)
                dve.tensor_reduce(st[:, 1, :], sq[:, :, :], AX_X, ALU.add).then_inc(s_var, 1)
                dve.wait_ge(s_sd, g + 1)
                step(dve.reciprocal(st[:, 3, :], st[:, 2, :]))
                dve.tensor_tensor(xc[:, u, :, :], xc[:, u, :, :], bc(st[:, 3, :], D), ALU.mult).then_inc(s_xn, 1)
                dve.wait_ge(s_lg, g + 1)
                lgp = lp[:, 0:G * E].rearrange("p (j e) -> p j e", e=E)
                step(dve.tensor_reduce(sc[:, 0, :], lgp, AX_X, ALU.max))
                dve.tensor_tensor(lg[:, :, :], lgp, bc(sc[:, 0, :], E), ALU.subtract).then_inc(s_ls, 1)
                dve.wait_ge(s_ls, g + 1)
                rk = rank[:, :].unsqueeze(1).to_broadcast([P, G, E])
                step(dve.tensor_scalar(tmp[:, :, :], lg[:, :, :], 0.0, None, ALU.is_ge))
                step(dve.tensor_tensor(tmp[:, :, :], tmp[:, :, :], rk, ALU.mult))
                step(dve.tensor_reduce(sc[:, 1, :], tmp[:, :, :], AX_X, ALU.max))
                step(dve.tensor_tensor(oh[:, :, :], rk, bc(sc[:, 1, :], E), ALU.is_equal))
                dve.tensor_copy(ohb[:, :, :], oh[:, :, :]).then_inc(s_oh, 1)
                dve.wait_ge(s_ex, g + 1)
                step(dve.tensor_reduce(sc[:, 2, :], ex[:, :, :], AX_X, ALU.add))
                step(dve.reciprocal(sc[:, 3, :], sc[:, 2, :]))
                step(dve.tensor_tensor(tmp[:, :, :], oh[:, :, :], ebase[:, :].unsqueeze(1).to_broadcast([P, G, E]),
                                       ALU.mult))
                step(dve.tensor_reduce(sc[:, 4, :], tmp[:, :, :], AX_X, ALU.add))
                dve.wait_ge(s_pos, g + 1)
                step(dve.tensor_tensor(tmp[:, :, :], cp[:, 0:G * E].rearrange("p (j e) -> p j e", e=E),
                                       carry[:, :].unsqueeze(1).to_broadcast([P, G, E]), ALU.add))
                step(dve.tensor_tensor(carry[:, :], cp[:, G * E:(G + 1) * E], carry[:, :], ALU.add))
                step(dve.tensor_tensor(tmp[:, :, :], tmp[:, :, :], oh[:, :, :], ALU.mult))
                step(dve.tensor_reduce(sc[:, 5, :], tmp[:, :, :], AX_X, ALU.add))
                step(dve.tensor_scalar(sc[:, 6, :], sc[:, 5, :], float(CAP), None, ALU.is_le))
                dve.tensor_tensor(k["weight"][:, bass.ds(g * G, G)], sc[:, 3, :], sc[:, 6, :], ALU.mult)
                step(dve.tensor_scalar(sc[:, 7, :], sc[:, 5, :], float(CAP), -1.0, ALU.min, ALU.add))
                dve.tensor_tensor(k["slot"][:, bass.ds(g * G, G)], sc[:, 7, :], sc[:, 4, :], ALU.add)
                tr = trash[:, bass.ds(g * G, G)]
                step(dve.tensor_tensor(sc[:, 5, :], sc[:, 7, :], sc[:, 4, :], ALU.add))
                step(dve.tensor_tensor(sc[:, 5, :], sc[:, 5, :], tr, ALU.subtract))
                step(dve.tensor_tensor(sc[:, 5, :], sc[:, 5, :], sc[:, 6, :], ALU.mult))
                dve.tensor_tensor(slot[:, u, :], sc[:, 5, :], tr, ALU.add).then_inc(s_slot, 1)
                assert m[0] == NV, m[0]

            groups(dve, body)


def experts(nc, ident, w1, b1, w2, b2, xe_dram, ye_dram, sem):
    JT = CAP // P
    FT = F // P
    HALF = CAP // 2
    with ExitStack() as ctx:
        def sb(name, shape, dt=F32):
            return ctx.enter_context(nc.sbuf_tensor(name, shape, dt))
        w1s = sb("w1s", [P, 2, KD_, F])
        w2s = sb("w2s", [P, 2, FT, D])
        b1s = sb("b1s", [P, 2, FT])
        b2s = sb("b2s", [1, 2, D])
        one = sb("d_one", [1, P])
        xe = sb("xe", [P, 2, JT, D])
        xT = sb("d_xT", [P, KD_, CAP])
        hT = sb("hT", [P, FT, CAP])
        ye = sb("ye", [P, 2, JT, D])
        tp = ctx.enter_context(nc.psum_tensor("d_tp", [P, 2, 512], F32))
        hp = ctx.enter_context(nc.psum_tensor("hp", [P, 4, 512], F32))
        yp = ctx.enter_context(nc.psum_tensor("yp", [P, 2, 512], F32))
        s_in = [sem(f"d_in{u}") for u in range(2)]
        s_out = [sem(f"d_out{u}") for u in range(2)]
        s_one, s_tr, s_xt, s_h, s_g, s_y, s_ye = (
            sem("d_" + n) for n in ("one", "tr", "xt", "h", "g", "y", "ye"))
        NL = 5 * 16
        NTR = KD_ * JT // 4
        NH2 = 2 * FT
        block = ctx.enter_context(nc.Block())

        @block.sync
        def _(sp):
            def load(e, u):
                def one_of(a):
                    return a[bass.ds(e, 1)]
                sp.dma_start(xe[:, u, :, :], xe_dram[bass.ds(e * CAP, CAP), :].rearrange(
                    "(j p) d -> p j d", p=P)).then_inc(s_in[u], 16)
                sp.dma_start(w1s[:, u, :, :], one_of(w1).rearrange("a (k p) f -> p (a k) f", p=P)
                             ).then_inc(s_in[u], 16)
                sp.dma_start(b1s[:, u, :], one_of(b1).rearrange("a (f p) -> p (a f)", p=P),
                             allow_slow_non_contiguous=True).then_inc(s_in[u], 16)
                sp.dma_start(w2s[:, u, :, :], one_of(w2).rearrange("a (f p) d -> p (a f) d", p=P)
                             ).then_inc(s_in[u], 16)
                sp.dma_start(b2s[:, u, :], one_of(b2)).then_inc(s_in[u], 16)

            load(0, 0)
            load(1, 1)
            with sp.Fori(0, E // 2 - 1) as i:
                for u in range(2):
                    sp.wait_ge(s_y, i * (2 * JT) + (u + 1) * JT)
                    load(i * 2 + (u + 2), u)

        @block.tensor
        def _(pe):
            pe.wait_ge(s_one, 1)
            with pe.Fori(0, E // 2) as i:
                for u in range(2):
                    e = i * 2 + u
                    pe.wait_ge(s_in[u], i * NL + NL)
                    for q in range(NTR):
                        pe.wait_ge(s_xt, e * NTR + (q + 1))
                        for j4 in range(4):
                            kk, j = divmod(4 * q + j4, JT)
                            mm = pe.transpose(tp[:, q % 2, j4 * P:(j4 + 1) * P],
                                              xe[:, u, j, kk * P:(kk + 1) * P], ident[:, :])
                        mm.then_inc(s_tr, 1)
                    pe.wait_ge(s_xt, e * NTR + (NTR + 2))
                    for f in range(FT):
                        for half in range(2):
                            q = 2 * f + half
                            pe.wait_ge(s_g, e * NH2 + (q + 1))
                            for kk in range(KD_):
                                mm = pe.matmul(hp[:, q % 4, 0:HALF], w1s[:, u, kk, f * P:(f + 1) * P],
                                               xT[:, kk, half * HALF:(half + 1) * HALF],
                                               start=(kk == 0), stop=(kk == KD_ - 1))
                            mm.then_inc(s_h, 1)
                    pe.wait_ge(s_g, e * NH2 + (NH2 + 4))
                    for j in range(JT):
                        pe.wait_ge(s_ye, e * JT + (j + 1))
                        for f in range(FT):
                            pe.matmul(yp[:, j % 2, 0:D], hT[:, f, j * P:(j + 1) * P], w2s[:, u, f, :],
                                      start=(f == 0), stop=False)
                        pe.matmul(yp[:, j % 2, 0:D], one[:, :], b2s[:, u, :], start=False,
                                  stop=True).then_inc(s_y, 1)

        @block.scalar
        def _(act):
            act.sem_inc(s_g, 4)
            with act.Fori(0, E // 2) as i:
                for u in range(2):
                    e = i * 2 + u
                    for q in range(NH2):
                        f, half = divmod(q, 2)
                        act.wait_ge(s_h, e * NH2 + (q + 1))
                        act.activation(hT[:, f, half * HALF:(half + 1) * HALF], hp[:, q % 4, 0:HALF],
                                       ACT.Gelu, bias=b1s[:, u, f:f + 1]).then_inc(s_g, 1)
                    act.wait_ge(s_ye, e * JT + (JT + 2))
                    act.dma_start(ye_dram[bass.ds(e * CAP, CAP), :].rearrange("(j p) d -> p j d", p=P),
                                  ye[:, u, :, :]).then_inc(s_out[u], 16)
            for u in range(2):
                act.wait_ge(s_out[u], 16 * (E // 2 + 1))

        @block.vector
        def _(dve):
            dve.memset(one[:, :], 1.0).then_inc(s_one, 1)
            dve.sem_inc(s_xt, 2)
            dve.sem_inc(s_ye, 2)
            for u in range(2):
                dve.sem_inc(s_out[u], 16)
            with dve.Fori(0, E // 2) as i:
                for u in range(2):
                    e = i * 2 + u
                    xTf = xT[:, :, :].rearrange("p k r -> p (k r)")
                    for q in range(NTR):
                        dve.wait_ge(s_tr, e * NTR + (q + 1))
                        dve.tensor_copy(xTf[:, q * 512:(q + 1) * 512], tp[:, q % 2, :]).then_inc(s_xt, 1)
                    dve.wait_ge(s_out[u], i * 16 + 16)
                    for j in range(JT):
                        dve.wait_ge(s_y, e * JT + (j + 1))
                        dve.tensor_copy(ye[:, u, j, :], yp[:, j % 2, 0:D]).then_inc(s_ye, 1)


def combine(nc, k, ye_dram, out, sem):
    Q = 4
    QN = NT // Q
    with ExitStack() as ctx:
        yr = ctx.enter_context(nc.sbuf_tensor("yr", [P, NT, D], F32))
        s_y = [sem(f"f_y{q}") for q in range(Q)]
        s_m, s_a, s_o = sem("f_m"), sem("f_a"), sem("f_o")
        out_v = out.rearrange("b (s p) d -> p (b s) d", p=P)
        block = ctx.enter_context(nc.Block())

        @block.gpsimd
        def _(pool):
            for j in range(NT):
                pool.indirect_dma_start(yr[:, j, :], None, ye_dram,
                                        bass.IndirectOffsetOnAxis(ap=k["slot"][:, j:j + 1], axis=0)
                                        ).then_inc(s_y[j // QN], 16)

        @block.vector
        def _(dve):
            for q in range(Q):
                qs = slice(q * QN, (q + 1) * QN)
                dve.wait_ge(s_y[q], 16 * QN)
                dve.tensor_tensor(yr[:, qs, :], yr[:, qs, :],
                                  k["weight"][:, qs].unsqueeze(2).to_broadcast([P, QN, D]),
                                  ALU.mult).then_inc(s_m, 1)
                dve.wait_ge(s_m, q + 1)
                dve.tensor_tensor(yr[:, qs, :], yr[:, qs, :], k["h2"][:, qs, :], ALU.add).then_inc(s_a, 1)

        @block.sync
        def _(sp):
            for q in range(Q):
                qs = slice(q * QN, (q + 1) * QN)
                sp.wait_ge(s_a, q + 1)
                sp.dma_start(out_v[:, qs, :], yr[:, qs, :]).then_inc(s_o, 16)
            sp.wait_ge(s_o, 16 * Q)


_INS = ['x', 'L0_tok_w', 'L0_attn_Wq', 'L0_attn_Wk', 'L0_attn_Wv', 'L0_attn_Wb', 'L0_attn_Wa',
        'L0_attn_A_log', 'L0_attn_dt_bias', 'L0_attn_conv_q', 'L0_attn_conv_k', 'L0_attn_conv_v',
        'L0_attn_Wg', 'L0_attn_rms_weight', 'L0_attn_Wo', 'L0_ffn_router_w', 'L0_ffn_w1', 'L0_ffn_b1',
        'L0_ffn_w2', 'L0_ffn_b2']


def kernel(**inputs):
    import numpy as np
    import concourse.bacc as bacc
    from concourse.bass_utils import run_bass_kernel_spmd

    nc = bacc.Bacc("TRN2", target_bir_lowering=False, num_devices=1)
    arrays, args = {}, []
    for name in _INS:
        a = np.ascontiguousarray(inputs[name])
        arrays[f"in_{name}"] = a
        args.append(nc.dram_tensor(f"in_{name}", a.shape, mybir.dt.from_np(a.dtype), kind="ExternalInput").ap())
    out = nc.dram_tensor("out_h", (B, T, D), F32, kind="ExternalOutput").ap()
    build(nc, *args, out)
    r = run_bass_kernel_spmd(nc, [arrays], core_ids=[0])
    return r.results[0]["out_h"]
```

```python
from contextlib import ExitStack

import concourse.bass as bass
from concourse import mybir

ALU = mybir.AluOpType
ACT = mybir.ActivationFunctionType
F32 = mybir.dt.float32
BF16 = mybir.dt.bfloat16
I32 = mybir.dt.int32
AX_X = mybir.AxisListType.X
P = 128

B, T, D = 16, 256, 256
N = B * T
H, HD, NH, CS = 8, 128, 3, 4
KD_ = D // P
E, F = 8, 1024
CAP = -(-3 * N // (2 * E))
C = 32
NC_ = T // C
R = NH * C
CB = B * C
IT = H * NC_
LEVELS = 5
TT = 2 * NH + 1
QT = NH
GATE = TT
G_MIN = -104.0
LN_EPS, L2_EPS, RMS_EPS = 1e-5, 1e-6, 1e-5
NT = N // P
TRASH = E * CAP

STREAM = [("d", 0), ("c", 0), ("c", 1), ("c", 2), ("kn", 0), ("kn", 1), ("c", 3), ("kn", 2),
          ("kn", 3), ("c", 4), ("vn", 0), ("c", 5), ("vn", 1), ("c", 6), ("vn", 2), ("vn", 3), ("g", 0)]
FIRST = [s for s in STREAM if s[0] in "dcg"]
N0, NS = len(FIRST), len(STREAM)
N_AFTER = [(1, 1), (1, 1), (1, 1), (1, 1), (1, 0)]


def build(nc, x, w_tok, wq, wk, wv, wb, wa, a_log, dt_bias, conv_q, conv_k, conv_v, wg,
          rms_weight, wo, router_w, w1, b1, w2, b2, out):
    with ExitStack() as ctx:
        def sem(name):
            return ctx.enter_context(nc.semaphore(name))

        h_dram = nc.dram_tensor("h_dram", [N, D], F32, kind="Internal").ap()
        o_dram = nc.dram_tensor("o_dram", [H, P, B, T], F32, kind="Internal").ap()
        xe_dram = nc.dram_tensor("xe_dram", [TRASH + N, D], F32, kind="Internal").ap()
        ye_dram = nc.dram_tensor("ye_dram", [TRASH, D], F32, kind="Internal").ap()

        ident = ctx.enter_context(nc.sbuf_tensor("ident", [P, P], F32))
        with ExitStack() as attn:
            def sb(name, shape, dt=F32):
                return attn.enter_context(nc.sbuf_tensor(name, shape, dt))
            t = {}
            t["xnT"] = sb("xnT", [P, KD_, NC_, CB])
            t["glog"] = sb("glog", [C, (IT + 1) * B])
            t["beta"] = sb("beta", [R, IT * B])
            t["neg_eg"] = sb("neg_eg", [R, IT * B])
            t["keep"] = sb("keep", [P, IT + 1])
            t["start"] = sb("start", [P, IT + 1])
            t["tri"] = sb("tri", [C, C])
            t["suf3"] = sb("suf3", [C, P])
            t["ones"] = sb("ones", [P, P])
            t["one_d"] = sb("one_d", [P, P])
            t["dmask"] = sb("dmask", [R, NH + 1, C])
            t["mask0"] = sb("mask0", [R, R])
            t["lmask"] = sb("lmask", [R, LEVELS, R // 2])
            t["eps_rms"] = sb("eps_rms", [P, 1])
            head = {"wq": wq, "wk": wk, "wv": wv, "wg": wg,
                    "conv_q": conv_q, "conv_k": conv_k, "conv_v": conv_v, "loaded": sem("m_w"),
                    "w_h": sb("w_h", [P, KD_, TT + 1, P]), "cw": sb("cw", [P, TT, CS])}
            embed(nc, t, head, ident, x, w_tok, wb, wa, a_log, dt_bias, h_dram, xe_dram, sem)
            attention(nc, t, head, ident, o_dram, sem)
        k = {"h2": ctx.enter_context(nc.sbuf_tensor("h2", [P, NT, D], F32)),
             "weight": ctx.enter_context(nc.sbuf_tensor("weight", [P, NT], F32)),
             "slot": ctx.enter_context(nc.sbuf_tensor("slot_of", [P, NT], I32))}
        ex = {"w1": w1, "b1": b1, "w2": w2, "b2": b2, "loaded": [sem(f"d_w{u}") for u in range(2)]}
        for name, shape in (("w1s", [P, 2, KD_, F]), ("w2s", [P, 2, F // P, D]), ("b1s", [P, 2, F // P]),
                            ("b2s", [P, 2, D])):
            ex[name] = ctx.enter_context(nc.sbuf_tensor(name, shape, F32))
        project_and_route(nc, k, ex, ident, wo, rms_weight, router_w, h_dram, o_dram, xe_dram, sem)
        experts(nc, ex, ident, xe_dram, ye_dram, sem)
        combine(nc, k, ye_dram, out, sem)


def load_head(sp, a, h):
    for k in range(KD_):
        rowsl = slice(k * P, (k + 1) * P)
        for src, t0, n in ((a["wk"], 0, NH), (a["wv"], NH + 1, NH)):
            v = src[rowsl, :].rearrange("p (i h c) -> p i h c", i=NH, h=H)
            for i in range(NH):
                sp.dma_start(a["w_h"][:, k, t0 + i, :], v[:, i, bass.ds(h, 1), :].rearrange(
                    "p a c -> p (a c)")).then_inc(a["loaded"], 16)
        for src, t0 in ((a["wq"], QT), (a["wg"], GATE)):
            v = src[rowsl, :].rearrange("p (h c) -> p h c", h=H)
            sp.dma_start(a["w_h"][:, k, t0, :], v[:, bass.ds(h, 1), :].rearrange(
                "p a c -> p (a c)")).then_inc(a["loaded"], 16)
    for src, t0, n in ((a["conv_k"], 0, NH), (a["conv_q"], QT, 1), (a["conv_v"], NH + 1, NH)):
        v = src.rearrange("(i h p) w -> p i h w", i=n, h=H)
        sp.dma_start(a["cw"][:, t0:t0 + n, :], v[:, :, bass.ds(h, 1), :].rearrange(
            "p i a w -> p i (a w)"), allow_slow_non_contiguous=True).then_inc(a["loaded"], 16)


def embed(nc, t, head, ident, x, w_tok, wb, wa, a_log, dt_bias, h_dram, xe_dram, sem):
    QN = 4
    QT_ = NT // QN
    with ExitStack() as ctx:
        def sb(name, shape, dt=F32):
            return ctx.enter_context(nc.sbuf_tensor(name, shape, dt))
        ids = sb("ids", [P, NT], I32)
        rows = sb("rows", [P, NT, D])
        xn = sb("xn", [P, NT, D])
        sq = sb("sq", [P, QT_, D])
        stat = sb("stat", [P, 4, NT])
        eps_ln = sb("eps_ln", [P, 1])
        zrow = sb("zrow", [P, CAP * E // P // 4, D])
        wab = sb("wab", [P, KD_, C])
        gates = xn[0:C, 0:16, :].rearrange("p a b -> p (a b)")
        gatesT = xn[0:C, 16:32, :].rearrange("p a b -> p (a b)")
        gt3 = gatesT.rearrange("p (m ch) -> p m ch", ch=C)
        tri3 = sb("tri3", [C, R])
        dtb = sb("dtb", [C, H])
        alog = sb("alog", [C, H])
        expa = sb("expa", [C, H])
        one32 = sb("one32", [C, 1])
        soft = sb("soft", [C, 5, H * P])
        lm = sb("lm", [C, LEVELS, R // 2])
        dm = sb("dm", [C, NH, NH + 1, C])
        m0 = sb("m0", [C, NH, R])
        pt = ctx.enter_context(nc.psum_tensor("pt", [P, 4, 512], F32))
        pg = ctx.enter_context(nc.psum_tensor("pg", [P, 2, 512], F32))

        s_ids = sem("e_ids")
        s_small = sem("e_small")
        s_rows = [sem(f"e_rows{q}") for q in range(QN)]
        s_hstore = sem("e_hstore")
        s_zero = sem("e_zero")
        s_cst = sem("e_cst")
        s_v = sem("e_v")
        s_cent = sem("e_cent")
        s_sq = sem("e_sq")
        s_var = sem("e_var")
        s_sd = sem("e_sd")
        s_xn = sem("e_xn")
        s_tr = sem("e_tr")
        s_xt = sem("e_xt")
        s_g = sem("e_g")
        s_gc = sem("e_gc")
        s_gv = sem("e_gv")
        s_ga = sem("e_ga")
        s_eg = sem("e_eg")
        s_lm = sem("e_lm")
        s_beta = sem("e_beta")
        xv = t["xnT"].rearrange("p k c (b t) -> p k c b t", b=B)
        n_gl = H * P

        block = ctx.enter_context(nc.Block())

        @block.sync
        def _(sp):
            sp.dma_start(ids[:, :], x.rearrange("b (s p) -> p (b s)", p=P),
                         allow_slow_non_contiguous=True).then_inc(s_ids, 16)
            for k in range(KD_):
                sp.dma_start(wab[:, k, 0:H * NH], wb[k * P:(k + 1) * P, :]).then_inc(s_small, 16)
                sp.dma_start(wab[:, k, H * NH:], wa[k * P:(k + 1) * P, :]).then_inc(s_small, 16)
            sp.dma_start(dtb[:, :], dt_bias.unsqueeze(0).to_broadcast([C, H])).then_inc(s_small, 16)
            sp.dma_start(alog[:, :], a_log.unsqueeze(0).to_broadcast([C, H])).then_inc(s_small, 16)
            load_head(sp, head, 0)
            for q in range(QN):
                sp.wait_ge(s_rows[q], 16 * QT_)
                sp.dma_start(h_dram[q * QT_ * P:(q + 1) * QT_ * P, :].rearrange("(j p) d -> p j d", p=P),
                             rows[:, q * QT_:(q + 1) * QT_, :]).then_inc(s_hstore, 16)
            sp.wait_ge(s_zero, 1)
            for q in range(4):
                n = CAP * E // 4
                sp.dma_start(xe_dram[q * n:(q + 1) * n, :].rearrange("(p j) d -> p j d", p=P),
                             zrow[:, :, :]).then_inc(s_hstore, 16)
            sp.wait_ge(s_hstore, 16 * (QN + 4))

        @block.gpsimd
        def _(pool):
            pool.wait_ge(s_ids, 16)
            for j in range(NT):
                pool.indirect_dma_start(rows[:, j, :], None, w_tok,
                                        bass.IndirectOffsetOnAxis(ap=ids[:, j:j + 1], axis=0)
                                        ).then_inc(s_rows[j // QT_], 16)
            cnt = [0]

            def step(ins):
                cnt[0] += 1
                ins.then_inc(s_cst, 1)
                pool.wait_ge(s_cst, cnt[0])

            def sel(ap, pattern, base, cm, op):
                step(pool.affine_select(out=ap, in_=ap, compare_op=op, fill=0.0, base=base,
                                        pattern=pattern, channel_multiplier=cm))

            step(pool.memset(ident[:, :], 1.0))
            sel(ident[:, :], [[-1, P]], 0, 1, ALU.is_equal)
            step(pool.memset(t["tri"][:, :], 1.0))
            sel(t["tri"][:, :], [[1, C]], 0, -1, ALU.is_ge)
            step(pool.memset(tri3[:, :], 1.0))
            sel(tri3[:, :], [[0, NH], [1, C]], 0, -1, ALU.is_ge)
            step(pool.memset(t["suf3"][:, :], 1.0))
            sel(t["suf3"][:, 0:R], [[0, NH], [-1, C]], 0, 1, ALU.is_gt)
            step(pool.memset(lm[:, :, :], 1.0))
            for lev in range(LEVELS):
                w = 1 << lev
                nb = C // (2 * w)
                sel(lm[:, lev, :], [[0, NH], [-2 * w, nb], [0, w]], -w, 1, ALU.is_ge)
                sel(lm[:, lev, :], [[0, NH], [2 * w, nb], [0, w]], 2 * w - 1, -1, ALU.is_ge)
            step(pool.memset(dm[:, :, 0:NH, :], -1.0))
            step(pool.memset(dm[:, :, NH, :], 1.0))
            step(pool.memset(m0[:, :, :], 0.0))
            for i in range(NH):
                sel(dm[:, i, 0:i + 1, :], [[0, i + 1], [1, C]], 0, -1, ALU.is_gt)
                sel(dm[:, i, i + 1:, :], [[0, NH - i], [1, C]], 0, -1, ALU.is_ge)
                if i < NH - 1:
                    later = m0[:, i, C * (i + 1):]
                    step(pool.memset(later, 1.0))
                    sel(later, [[0, NH - 1 - i], [1, C]], 0, -1, ALU.is_equal)
            pool.drain().then_inc(s_lm, 1)

        @block.vector
        def _(dve):
            done = [0]

            def step(ins):
                done[0] += 1
                ins.then_inc(s_v, 1)
                dve.wait_ge(s_v, done[0])

            dve.memset(zrow[:, :, :], 0.0).then_inc(s_zero, 1)
            step(dve.memset(eps_ln[:, :], LN_EPS))
            step(dve.memset(one32[:, :], 1.0))
            dve.memset(t["ones"][:, :], 1.0)
            dve.memset(t["one_d"][:, :], 1.0 / HD)
            dve.memset(t["eps_rms"][:, :], RMS_EPS * HD * L2_EPS)
            step(dve.memset(t["keep"][:, :], 1.0))
            step(dve.memset(t["start"][:, :], 0.0))
            dve.memset(t["keep"][:, ::NC_], 0.0)
            dve.memset(t["start"][R:, ::NC_], -1e30)
            dve.memset(t["glog"][:, IT * B:], 0.0)

            def centre(q):
                qs = slice(q * QT_, (q + 1) * QT_)
                dve.wait_ge(s_rows[q], 16 * QT_)
                step(dve.tensor_reduce(stat[:, 0, qs], rows[:, qs, :], AX_X, ALU.add))
                step(dve.tensor_scalar(stat[:, 0, qs], stat[:, 0, qs], -1.0 / D, None, ALU.mult))
                dve.tensor_tensor(xn[:, qs, :], rows[:, qs, :],
                                  stat[:, 0, qs].unsqueeze(2).to_broadcast([P, QT_, D]),
                                  ALU.add).then_inc(s_cent, 1)

            def scale(q):
                qs = slice(q * QT_, (q + 1) * QT_)
                dve.wait_ge(s_sq, q + 1)
                dve.tensor_reduce(stat[:, 1, qs], sq[:, :, :], AX_X, ALU.add).then_inc(s_var, 1)
                dve.wait_ge(s_sd, q + 1)
                step(dve.reciprocal(stat[:, 3, qs], stat[:, 2, qs]))
                dve.wait_ge(s_cent, q + 1)
                dve.tensor_tensor(xn[:, qs, :], xn[:, qs, :],
                                  stat[:, 3, qs].unsqueeze(2).to_broadcast([P, QT_, D]),
                                  ALU.mult).then_inc(s_xn, 1)

            centre(0)
            for q in range(1, QN):
                centre(q)
                scale(q - 1)
            scale(QN - 1)
            dve.wait_ge(s_lm, 1)
            for i in range(NH):
                step(dve.tensor_copy(t["lmask"][C * i:C * (i + 1), :, :], lm[:, :, :]))
                step(dve.tensor_copy(t["dmask"][C * i:C * (i + 1), :, :], dm[:, i, :, :]))
                step(dve.tensor_copy(t["mask0"][C * i:C * (i + 1), :], m0[:, i, :]))
            dve.wait_ge(s_gc, NC_)
            step(dve.transpose(gatesT, gates))
            dve.wait_ge(s_small, 16 * (2 * KD_ + 2))
            s3 = [soft[:, i, :].rearrange("p (h m) -> p h m", h=H) for i in range(5)]
            step(dve.tensor_tensor(s3[0], gt3[:, :, H * NH:].rearrange("p m h -> p h m"),
                                   dtb[:, :].unsqueeze(2).to_broadcast([C, H, P]), ALU.add))
            step(dve.tensor_scalar(soft[:, 1, :], soft[:, 0, :], -1.0, None, ALU.mult))
            dve.tensor_tensor(soft[:, 1, :], soft[:, 0, :], soft[:, 1, :], ALU.min).then_inc(s_gv, 1)
            beta = t["beta"].rearrange("p (h m) -> p h m", h=H)
            for i in range(NH):
                step(dve.tensor_copy(beta[C * i:C * (i + 1), :, :],
                                     gt3[:, :, H * i:H * (i + 1)].rearrange("p m h -> p h m")))
            dve.sem_inc(s_beta, 1)
            dve.wait_ge(s_ga, 2)
            step(dve.tensor_scalar(soft[:, 3, :], soft[:, 2, :], 1.0, None, ALU.add))
            dve.tensor_scalar(soft[:, 4, :], soft[:, 3, :], -1.0, None, ALU.add).then_inc(s_gv, 1)
            dve.wait_ge(s_gv, 2)
            step(dve.tensor_tensor(soft[:, 4, :], soft[:, 2, :], soft[:, 4, :], ALU.subtract))
            dve.wait_ge(s_ga, 3)
            step(dve.reciprocal(soft[:, 2, :], soft[:, 3, :]))
            step(dve.tensor_tensor(soft[:, 4, :], soft[:, 4, :], soft[:, 2, :], ALU.mult))
            step(dve.tensor_tensor(soft[:, 4, :], soft[:, 4, :], soft[:, 1, :], ALU.add))
            step(dve.scalar_tensor_tensor(out=soft[:, 4, :], in0=soft[:, 0, :], scalar=0.0,
                                          in1=soft[:, 4, :], op0=ALU.max, op1=ALU.add))
            step(dve.tensor_scalar(expa[:, :], expa[:, :], -1.0, None, ALU.mult))
            step(dve.tensor_tensor(s3[4], s3[4], expa[:, :].unsqueeze(2).to_broadcast([C, H, P]),
                                   ALU.mult))
            dve.tensor_scalar(t["glog"][:, 0:n_gl], soft[:, 4, :], G_MIN, None, ALU.max).then_inc(s_gv, 1)
            dve.wait_ge(s_ga, 4)
            step(dve.tensor_scalar(t["beta"][:, :], t["beta"][:, :], 0.5, 0.5, ALU.mult, ALU.add))
            step(dve.reciprocal(t["beta"][:, :], t["beta"][:, :]))
            dve.wait_ge(s_eg, 2)
            step(dve.tensor_scalar(t["neg_eg"][:, :], t["neg_eg"][:, :], -1.0, None, ALU.mult))
            step(dve.memset(t["neg_eg"].rearrange("p (h m) -> p h m", h=H)[:, :, 0:B], 0.0))

        @block.scalar
        def _(act):
            def evac(m):
                act.wait_ge(s_tr, m + 1)
                k, j4 = m % 2, m // 2
                act.copy(xv[:, k, 0:NC_, 2 * j4:2 * j4 + 2, :].rearrange("p c b t -> p b c t"),
                         pt[:, m % 4, :].rearrange("p (b c t) -> p b c t", b=2, c=NC_)).then_inc(s_xt, 1)

            for q in range(QN):
                qs = slice(q * QT_, (q + 1) * QT_)
                act.wait_ge(s_cent, q + 1)
                act.activation(sq[:, :, :], xn[:, qs, :], ACT.Square).then_inc(s_sq, 1)
                if q > 0:
                    for m in range((q - 1) * QT_ // 2, q * QT_ // 2):
                        evac(m)
                act.wait_ge(s_var, q + 1)
                act.activation(stat[:, 2, qs], stat[:, 1, qs], ACT.Sqrt, bias=eps_ln[:, :],
                               scale=1.0 / D).then_inc(s_sd, 1)
            for m in range((QN - 1) * QT_ // 2, QN * QT_ // 2):
                evac(m)
            for c in range(NC_):
                act.wait_ge(s_g, c + 1)
                act.copy(gates[:, c * CB:(c + 1) * CB], pg[0:C, c % 2, :]).then_inc(s_gc, 1)
            act.wait_ge(s_small, 16 * (2 * KD_ + 2))
            act.activation(expa[:, :], alog[:, :], ACT.Exp).then_inc(s_ga, 1)
            act.wait_ge(s_gv, 1)
            act.activation(soft[:, 2, :], soft[:, 1, :], ACT.Exp).then_inc(s_ga, 1)
            act.wait_ge(s_ga, 2)
            act.activation(soft[:, 1, :], soft[:, 2, :], ACT.Ln, bias=one32[:, :]).then_inc(s_ga, 1)
            act.wait_ge(s_beta, 1)
            act.activation(t["beta"][:, :], t["beta"][:, :], ACT.Exp, scale=-1.0).then_inc(s_ga, 1)
            for m in range(2):
                act.wait_ge(s_g, NC_ + m + 1)
                act.activation(t["neg_eg"][:, m * 512:(m + 1) * 512], pg[0:R, m, :],
                               ACT.Exp).then_inc(s_eg, 1)

        @block.tensor
        def _(pe):
            for m in range(2 * NT // 4):
                k, j4 = m % 2, m // 2
                if m % (QT_ // 2) == 0:
                    pe.wait_ge(s_xn, m // (QT_ // 2) + 1)
                if m == 0:
                    pe.wait_ge(s_cst, 2)
                if m >= 4:
                    pe.wait_ge(s_xt, m - 3)
                for j in range(4):
                    last = pe.transpose(pt[:, m % 4, j * P:(j + 1) * P],
                                        xn[:, 4 * j4 + j, k * P:(k + 1) * P], ident[:, :])
                last.then_inc(s_tr, 1)
            pe.wait_ge(s_xt, 2 * NT // 4)
            pe.wait_ge(s_small, 16 * (2 * KD_ + 2))
            for c in range(NC_):
                if c >= 2:
                    pe.wait_ge(s_gc, c - 1)
                for k in range(KD_):
                    mm = pe.matmul(pg[0:C, c % 2, :], wab[:, k, :], t["xnT"][:, k, c, :],
                                   start=(k == 0), stop=(k == KD_ - 1))
                mm.then_inc(s_g, 1)
            pe.wait_ge(s_gv, 3)
            pe.wait_ge(s_gc, NC_)
            pe.wait_ge(s_lm, 1)
            for m in range(2):
                pe.matmul(pg[0:R, m, :], tri3[:, :], t["glog"][:, m * 512:(m + 1) * 512],
                          start=True, stop=True).then_inc(s_g, 1)


def attention(nc, t, head, ident, o_dram, sem):
    with ExitStack() as ctx:
        def sb(name, shape, dt=F32):
            return ctx.enter_context(nc.sbuf_tensor(name, shape, dt))
        w_h, cw = head["w_h"], head["cw"]
        raw = sb("raw", [P, TT, B, C + CS - 1])
        cv = sb("cv", [P, TT, B, C])
        kq = sb("kq", [P, B, NH + 1, C])
        vq = sb("vq", [P, B, NH, C])
        ksq = sb("ksq", [P, B, NH, C])
        qsq = sb("qsq", [P, CB])
        gtri = sb("gtri", [C, B, C])
        ed = sb("ed", [P, B, C])
        sdn = sb("sdn", [P, B])
        dt_ = sb("dt_", [R, B, NH + 1, C])
        up = sb("up", [P, B, NH + 1, C])
        u0 = sb("u0", [R, B, R])
        zt = sb("zt", [R, B, R])
        yt = sb("yt", [R, B, R])
        p2 = sb("p2", [R, B, R // 2])
        p2l = sb("p2l", [R, B, R])
        state = sb("state", [P, B, HD])
        vs = sb("vs", [R, B, HD])
        kd = sb("kd", [R, B, HD])
        xs = sb("xs", [P, B, HD])
        gate_n = sb("gate_n", [P, CB])
        gate = sb("gate", [P, CB])
        osq = sb("osq", [P, CB])
        rt = sb("rt", [P, CB])
        og = sb("og", [P, CB])
        sm = sb("sm", [R, 6, B])
        sdec = sb("sdec", [P, B])
        tok = sb("tok", [C, 2, B])
        tok2 = sb("tok2", [C, B // 2, C])
        ps = lambda name, shape: ctx.enter_context(nc.psum_tensor(name, shape, F32))
        pj = ps("pj", [P, 2, 512])
        wa_ = ps("wa_", [P, 512])
        wb_ = ps("wb_", [P, 512])
        tb = ps("tb", [P, 2, 512])
        ta = ps("ta", [P, 2, 512])
        GW = [wa_, wb_]
        GT = [ta, tb]
        KKB = [wa_, wb_, tb[:, 0, :], tb[:, 1, :]]
        KSB = [tb[:, 0, :], tb[:, 1, :], ta[:, 0, :], ta[:, 1, :]]
        XB = [wa_, wb_, tb[:, 0, :], tb[:, 1, :]]
        SUB = [ta[:, 1, :], wa_, wb_, tb[:, 0, :]]
        o_ps, rms_ps, n_ps, s_ps = ta[:, 0, :], tb[:, 1, :], ta[:, 1, :], ta[:, 1, B:2 * B]

        S = {n: sem("m_" + n) for n in (
            "item", "item_out", "norm", "kkp", "z0t", "qs", "tok", "p2", "zn", "ytt", "ks", "x",
            "o", "su", "rms", "small", "up", "y0", "p2m", "zadd", "r", "state", "halo", "conv", "rr",
            "t1", "sn", "z0", "y", "xo", "silu", "osq", "oqs", "rt", "gtri", "dt", "ksq", "qsq",
            "gate", "dsum", "sdn", "u0", "yi", "og", "stored", "passed")}
        S["w"] = head["loaded"]
        W_DMAS = 2 * 8 + 3
        NSM = 7
        NCV = (CS - 1) * TT
        NTOK = 4

        def lo_hi(ap3, lev, half):
            w = 1 << lev
            return ap3.rearrange("p b (m two w) -> p b m two w", two=2, w=w)[:, :, :, half, :]

        block = ctx.enter_context(nc.Block())

        @block.sync
        def _(sp):
            def store(h, c, it):
                sp.wait_ge(S["og"], it + 2)
                sp.dma_start(o_dram[bass.ds(h, 1), :, :, bass.ds(c * C, C)].rearrange("a p b t -> (a p) b t"),
                             og[:, :].rearrange("p (b t) -> p b t", b=B)).then_inc(S["stored"], 16)

            sp.sem_inc(S["stored"], 32)
            with sp.Fori(0, H - 1) as h:
                with sp.Fori(0, NC_ - 1) as c:
                    store(h, c, h * NC_ + c)
                load_head(sp, head, h + 1)
                store(h, NC_ - 1, h * NC_ + NC_ - 1)
            with sp.Fori(0, NC_ - 1) as c:
                store(H - 1, c, (H - 1) * NC_ + c)
            load_head(sp, head, 0)
            store(H - 1, NC_ - 1, IT - 1)
            sp.wait_ge(S["stored"], 16 * (IT + 2))
            sp.wait_ge(S["w"], 16 * W_DMAS * (H + 1))

        @block.tensor
        def _(pe):
            def item(kind, a, base, k, it, chunk):
                bank = pj[:, k % 2, :]
                if not (it is None and k < 2):
                    pe.wait_ge(S["item_out"], base + k - 1)
                if kind == "d":
                    pe.wait_ge(S["gtri"], 1 if it is None else it + 2)
                    mm = pe.matmul(bank, t["suf3"][:, :], gtri[:, :, :], start=True, stop=True)
                elif kind in "cg":
                    tile = a if kind == "c" else GATE
                    for h2 in range(KD_):
                        mm = pe.matmul(bank, w_h[:, h2, tile, :], chunk(h2),
                                       start=(h2 == 0), stop=(h2 == KD_ - 1))
                else:
                    src = kq if kind == "kn" else vq
                    for j in range(4):
                        mm = pe.transpose(bank[0:R, j * HD:(j + 1) * HD],
                                          src[:, 4 * a + j, 0:NH, :], ident[:, :])
                mm.then_inc(S["item"], 1)

            def sum_chunk(nxt):
                pe.wait_ge(S["gtri"], nxt + 1)
                pe.matmul(s_ps, t["ones"][0:C, :], gtri[:, :, C - 1], start=True, stop=True
                          ).then_inc(S["dsum"], 1)

            sum_chunk(0)
            pe.wait_ge(S["w"], 16 * W_DMAS)
            for k, (kind, a) in enumerate(FIRST):
                item(kind, a, 0, k, None, lambda h2: t["xnT"][:, h2, 0, :])

            with pe.Fori(0, IT) as it:
                base = it * NS + N0
                nxt = (it + 1) % NC_

                def chunk(h2):
                    return t["xnT"][:, h2, bass.ds(nxt, 1), :].rearrange("p a c -> p (a c)")

                todo = [(k, *s) for k, s in enumerate(STREAM)]

                def stream(n):
                    for _ in range(n):
                        k, kind, a = todo.pop(0)
                        if kind == "c" and a == 0:
                            pe.wait_ge(S["w"], wneed)
                        item(kind, a, base, k, it, chunk)

                wneed = ((it + 1) // NC_ + 1) * (16 * W_DMAS)
                pe.wait_ge(S["ksq"], it + 1)
                pe.wait_ge(S["state"], it * 4 + 1)
                pe.wait_ge(S["sdn"], it + 1)
                sum_chunk(it + 1)
                for b in range(B):
                    mm = pe.matmul(n_ps[0:R, b:b + 1], ksq[:, b, :, :], t["ones"][:, 0:1],
                                   start=True, stop=True)
                mm.then_inc(S["norm"], 1)
                pe.wait_ge(S["silu"], (it + 1) * TT)
                for g in range(4):
                    if g == 3:
                        pe.wait_ge(S["sn"], it + 1)
                    else:
                        pe.wait_ge(S["state"], it * 4 + 2 + g)
                    for j in range(4):
                        b = 4 * g + j
                        mm = pe.matmul(KKB[g][0:R, j * P:(j + 1) * P], kq[:, b, 0:NH, :],
                                       kq[:, b, :, :], start=True, stop=True)
                    mm.then_inc(S["kkp"], 1)
                stream(5)
                for g in range(2):
                    if g == 1:
                        stream(1)
                    if g == 0:
                        pe.wait_ge(S["sdn"], it + 2)
                    pe.wait_ge(S["y0"], 2 * it + g + 1)
                    for j in range(8):
                        mm = pe.transpose(GT[g][0:R, j // 4, (j % 4) * P:(j % 4) * P + R],
                                          yt[:, 8 * g + j, :], ident[0:R, 0:R])
                    mm.then_inc(S["z0t"], 1)
                stream(2)
                for lev in range(LEVELS):
                    last = lev == LEVELS - 1
                    for g in range(2):
                        if lev == 0:
                            pe.wait_ge(S["z0"], 2 * it + g + 1)
                        else:
                            pe.wait_ge(S["zadd"], 2 * LEVELS * it + 2 * lev + g - 1)
                        for j in range(8):
                            b = 8 * g + j
                            mm = pe.matmul(GW[g][0:R, j * R // 2:(j + 1) * R // 2], up[0:R, b, 0:NH, :],
                                           lo_hi(zt, lev, 0)[:, b], start=True, stop=True)
                        mm.then_inc(S["p2"], 1)
                    stream(N_AFTER[lev][0])
                    for g in range(2):
                        pe.wait_ge(S["p2m"], 2 * LEVELS * it + 2 * lev + g + 1)
                        if lev > 0:
                            pe.wait_ge(S["y"], 2 * (LEVELS - 1) * it + 2 * lev + g - 1)
                        for j in range(8):
                            b = 8 * g + j
                            if last:
                                lhs, rhs = p2l[:, b, :], lo_hi(yt, lev, 1)[:, b]
                            else:
                                lhs, rhs = yt[:, b, :], p2[:, b, :]
                            mm = pe.matmul(GW[g][0:R, j * R // 2:(j + 1) * R // 2], lhs, rhs,
                                           start=True, stop=True)
                        mm.then_inc(S["zn"], 1)
                    stream(N_AFTER[lev][1])
                    if not last:
                        for g in range(2):
                            pe.wait_ge(S["zadd"], 2 * LEVELS * it + 2 * lev + g + 1)
                            for j in range(8):
                                mm = pe.transpose(GT[g][0:R, j // 4, (j % 4) * P:(j % 4) * P + R],
                                                  zt[:, 8 * g + j, :], ident[0:R, 0:R])
                            mm.then_inc(S["ytt"], 1)
                assert not todo
                for g in range(4):
                    for j in range(4):
                        b = 4 * g + j
                        mm = pe.matmul(KSB[g][:, j * HD:(j + 1) * HD], kq[:, b, :, :],
                                       state[:, b, :], start=True, stop=True)
                    mm.then_inc(S["ks"], 1)
                for g in range(4):
                    if g % 2 == 0:
                        pe.wait_ge(S["zadd"], 2 * LEVELS * it + 2 * LEVELS - 1 + g // 2)
                    pe.wait_ge(S["r"], 4 * it + g + 1)
                    if g >= 2:
                        pe.wait_ge(S["qs"], 4 * it + g - 1)
                    if g == 0:
                        pe.wait_ge(S["zadd"], 2 * LEVELS * (it + 1))
                    for j in range(4):
                        b = 4 * g + j
                        mm = pe.matmul(XB[g][0:R, j * HD:(j + 1) * HD], yt[:, b, :], vs[:, b, :],
                                       start=True, stop=True)
                    mm.then_inc(S["x"], 1)
                pe.wait_ge(S["qs"], 4 * (it + 1))
                pe.wait_ge(S["small"], NSM * (it + 1))
                for g in range(4):
                    pe.wait_ge(S["xo"], 4 * it + g + 1)
                    for j in range(4):
                        b = 4 * g + j
                        mm = pe.matmul(o_ps[:, b * C:(b + 1) * C], xs[:, b, :], up[:, b, NH, :],
                                       start=True, stop=True)
                mm.then_inc(S["o"], 1)
                for g in range(4):
                    for j in range(4):
                        b = 4 * g + j
                        mm = pe.matmul(SUB[g][:, j * HD:(j + 1) * HD], kd[:, b, :], xs[0:R, b, :],
                                       start=True, stop=True)
                    mm.then_inc(S["su"], 1)
                pe.wait_ge(S["oqs"], it + 1)
                pe.matmul(rms_ps, t["one_d"][:, :], osq[:, :], start=True, stop=True).then_inc(S["rms"], 1)

        @block.scalar
        def _(act):
            def item(kind, a, base, k, it):
                bank = pj[:, k % 2, :]
                nxt = 0 if it is None else it + 1
                act.wait_ge(S["item"], base + k + 1)
                if kind == "d":
                    if it is not None:
                        act.wait_ge(S["dt"], it + 1)
                        act.wait_ge(S["small"], NSM * (it + 1))
                    bias = t["start"][:, 0:1] if it is None else t["start"][:, bass.ds(nxt, 1)]
                    ins = act.activation(ed[:, :, :], bank, ACT.Exp, bias=bias)
                elif kind == "c":
                    if a == 0:
                        act.wait_ge(S["halo"], 1 if it is None else it + 2)
                    act.copy(raw[:, a, :, CS - 1:], bank)
                    ins = act.mul(cv[:, a, :, :], bank, cw[:, a, CS - 1:CS])
                elif kind == "g":
                    if it is not None:
                        act.wait_ge(S["gate"], it + 2)
                    ins = act.activation(gate_n[:, :], bank, ACT.Silu)
                elif kind == "kn":
                    if a == 0:
                        act.wait_ge(S["small"], NSM * (it + 1))
                    for j in range(4):
                        b = 4 * a + j
                        ins = act.mul(kd[:, b, :], bank[0:R, j * HD:(j + 1) * HD], sm[:, 3, b:b + 1])
                else:
                    for j in range(4):
                        b = 4 * a + j
                        ins = act.mul(vs[:, b, :], bank[0:R, j * HD:(j + 1) * HD], sm[:, 4, b:b + 1])
                ins.then_inc(S["item_out"], 1)

            def silu(tile, it):
                nxt = 0 if it is None else it + 1
                act.wait_ge(S["conv"], nxt * NCV + (CS - 1) * (tile + 1))
                dst = kq[:, :, tile, :] if tile <= QT else vq[:, :, tile - QT - 1, :]
                act.activation(dst, cv[:, tile, :, :], ACT.Silu).then_inc(S["silu"], 1)

            def chunk_decay(nxt):
                act.wait_ge(S["dsum"], nxt + 1)
                act.activation(sdn[:, :], s_ps, ACT.Exp).then_inc(S["sdn"], 1)

            chunk_decay(0)
            for k, (kind, a) in enumerate(FIRST):
                item(kind, a, 0, k, None)
            for tile in range(TT):
                silu(tile, None)

            with act.Fori(0, IT) as it:
                base = it * NS + N0
                todo = [(k, *s) for k, s in enumerate(STREAM)]

                def stream(n):
                    for _ in range(n):
                        k, kind, a = todo.pop(0)
                        item(kind, a, base, k, it)

                act.wait_ge(S["small"], NSM * it + 4)
                act.activation(sm[:, 4, :], sm[:, 0, :], ACT.Sqrt).then_inc(S["sn"], 1)
                act.wait_ge(S["sn"], it + 1)
                chunk_decay(it + 1)
                stream(5)
                for g in range(2):
                    if g == 1:
                        stream(1)
                    act.wait_ge(S["z0t"], 2 * it + g + 1)
                    act.copy(zt[:, 8 * g:8 * g + 8, :],
                             GT[g][0:R, :, :].rearrange("p k (j r) -> p (k j) r", r=P)[:, :, 0:R]
                             ).then_inc(S["z0"], 1)
                stream(2)
                for lev in range(LEVELS):
                    stream(N_AFTER[lev][0])
                    stream(N_AFTER[lev][1])
                    if lev < LEVELS - 1:
                        w = 1 << lev
                        for g in range(2):
                            act.wait_ge(S["ytt"], 2 * (LEVELS - 1) * it + 2 * lev + g + 1)
                            src = GT[g][0:R, :, :].rearrange("p k (j m two w) -> p (k j) m two w",
                                                            two=2, w=w, m=P // (2 * w))
                            act.copy(lo_hi(yt, lev, 1)[:, 8 * g:8 * g + 8],
                                     src[:, :, 0:R // (2 * w), 1, :]).then_inc(S["y"], 1)
                for g in range(4):
                    act.wait_ge(S["ks"], 4 * it + g + 1)
                    act.copy(xs[R:, 4 * g:4 * g + 4, :], KSB[g][R:, :]).then_inc(S["qs"], 1)
                for g in range(4):
                    act.wait_ge(S["x"], 4 * it + g + 1)
                    act.copy(xs[0:R, 4 * g:4 * g + 4, :], XB[g][0:R, :]).then_inc(S["xo"], 1)
                act.wait_ge(S["qsq"], 2 * it + 1)
                for tile in range(NH):
                    silu(tile, it)
                act.wait_ge(S["o"], it + 1)
                act.activation(osq[:, :], o_ps, ACT.Square).then_inc(S["osq"], 1)
                for tile in range(NH, TT):
                    silu(tile, it)
                act.wait_ge(S["rms"], it + 1)
                act.activation(rt[:, :], rms_ps, ACT.Sqrt, bias=t["eps_rms"][:, :]).then_inc(S["rt"], 1)

        @block.vector
        def _(dve):
            def halo(keep, n):
                dve.tensor_scalar(raw[:, :, :, 0:CS - 1].rearrange("p t b w -> p (t b) w"),
                                  raw[:, :, :, C:].rearrange("p t b w -> p (t b) w"),
                                  keep, None, ALU.mult).then_inc(S["halo"], 1)

            def conv(tile, it):
                base = 0 if it is None else it * NS + N0
                k = (FIRST if it is None else STREAM).index(("c", tile))
                nxt = 0 if it is None else it + 1
                dve.wait_ge(S["item_out"], base + k + 1)
                for i in range(CS - 2, -1, -1):
                    n = nxt * NCV + (CS - 1) * tile + (CS - 2 - i)
                    if i < CS - 2:
                        dve.wait_ge(S["conv"], n)
                    dve.scalar_tensor_tensor(out=cv[:, tile, :, :], in0=raw[:, tile, :, i:i + C],
                                             scalar=cw[:, tile, i:i + 1], in1=cv[:, tile, :, :],
                                             op0=ALU.mult, op1=ALU.add).then_inc(S["conv"], 1)

            def scale_outputs(n):
                dve.wait_ge(S["rt"], n + 1)
                dve.reciprocal(rt[:, :], rt[:, :]).then_inc(S["rr"], 1)
                dve.wait_ge(S["rr"], n + 1)
                dve.tensor_tensor(rt[:, :], o_ps, rt[:, :], ALU.mult).then_inc(S["t1"], 1)

            def make_ksq(nxt):
                dve.wait_ge(S["silu"], nxt * TT + NH)
                dve.tensor_tensor(ksq[:, :, :, :], kq[:, :, 0:NH, :], kq[:, :, 0:NH, :],
                                  ALU.mult).then_inc(S["ksq"], 1)

            dve.memset(p2l[:, :, :], 0.0)
            dve.memset(o_ps, 0.0)
            dve.memset(rt[:, :], 1.0).then_inc(S["rt"], 1)
            dve.memset(state[:, :, :], 0.0).then_inc(S["state"], 4)
            dve.memset(raw[:, :, :, 0:CS - 1], 0.0).then_inc(S["halo"], 1)
            dve.wait_ge(S["w"], 16 * W_DMAS)
            for tile in range(TT):
                conv(tile, None)
            make_ksq(0)

            with dve.Fori(0, IT) as it:
                base = it * NSM
                cols = bass.ds(it * B, B)
                dve.wait_ge(S["conv"], NCV * (it + 1))
                halo(t["keep"][:, bass.ds(it + 1, 1)], it)
                dve.tensor_tensor(up[R:, :, NH, :], ed[R:, :, :],
                                  ident[R:, R:].unsqueeze(1).to_broadcast([C, B, C]),
                                  ALU.mult).then_inc(S["small"], 1)
                dve.tensor_copy(sm[:, 5, :], t["neg_eg"][:, cols]).then_inc(S["small"], 1)
                dve.wait_ge(S["state"], 4 * (it + 1))
                dve.wait_ge(S["sdn"], it + 1)
                dve.tensor_scalar(sdec[:, :], sdn[:, :], t["keep"][:, bass.ds(it, 1)], None, ALU.mult
                                  ).then_inc(S["small"], 1)
                dve.wait_ge(S["norm"], it + 1)
                dve.tensor_scalar(sm[:, 0, :], n_ps[0:R, 0:B], L2_EPS, None, ALU.add).then_inc(S["small"], 1)
                dve.wait_ge(S["small"], base + 4)
                dve.reciprocal(sm[:, 1, :], sm[:, 0, :]).then_inc(S["small"], 1)
                dve.wait_ge(S["small"], base + 5)
                dve.tensor_tensor(sm[:, 2, :], sm[:, 1, :], t["beta"][:, cols], ALU.mult).then_inc(S["small"], 1)
                dve.wait_ge(S["small"], base + 6)
                dve.tensor_tensor(sm[:, 3, :], sm[:, 2, :], ed[0:R, :, C - 1], ALU.mult).then_inc(S["small"], 1)
                dve.wait_ge(S["dt"], it + 1)
                for g in range(4):
                    dve.wait_ge(S["kkp"], 4 * it + g + 1)
                    for j in range(4):
                        b = 4 * g + j
                        ins = dve.scalar_tensor_tensor(
                            out=up[0:R, b, :, :], in0=KKB[g][0:R, j * P:(j + 1) * P].rearrange(
                                "p (i c) -> p i c", c=C),
                            scalar=sm[:, 2, b:b + 1], in1=dt_[:, b, :, :], op0=ALU.mult, op1=ALU.mult)
                    ins.then_inc(S["up"], 1)
                for g in range(2):
                    bs = slice(8 * g, 8 * g + 8)
                    nt = NTOK * (2 * it + g)
                    dve.wait_ge(S["u0"], 2 * it + g + 1)
                    dve.tensor_reduce(tok[:, 0, bs], u0[0:C, bs, C:2 * C], AX_X, ALU.add).then_inc(S["tok"], 1)
                    dve.tensor_reduce(tok[:, 1, bs], u0[C:2 * C, bs, 2 * C:], AX_X, ALU.add
                                      ).then_inc(S["tok"], 1)
                    dve.wait_ge(S["tok"], nt + 2)
                    dve.tensor_tensor(tok[:, 0, bs], tok[:, 0, bs], tok[:, 1, bs], ALU.mult
                                      ).then_inc(S["tok"], 1)
                    dve.wait_ge(S["tok"], nt + 3)
                    dve.tensor_tensor(tok2[:, :, :], tok[:, 0, bs].unsqueeze(2).to_broadcast([C, 8, C]),
                                      ident[0:C, 0:C].unsqueeze(1).to_broadcast([C, 8, C]), ALU.mult
                                      ).then_inc(S["tok"], 1)
                    if g == 0:
                        scale_outputs(it)
                    dve.wait_ge(S["tok"], nt + 4)
                    dve.wait_ge(S["yi"], 2 * it + g + 1)
                    dve.tensor_tensor(yt[0:C, bs, 2 * C:], yt[0:C, bs, 2 * C:], tok2[:, :, :],
                                      ALU.add).then_inc(S["y0"], 1)
                conv(0, it)
                conv(1, it)
                for lev in range(LEVELS):
                    last = lev == LEVELS - 1
                    for g in range(2):
                        n = 2 * LEVELS * it + 2 * lev + g + 1
                        dve.wait_ge(S["p2"], n)
                        src = GW[g][0:R, 0:4 * R].rearrange("p (j c) -> p j c", j=8)
                        mask = t["lmask"][:, lev, :].unsqueeze(1).to_broadcast([R, 8, R // 2])
                        if last:
                            w = C // 2
                            dve.tensor_tensor(
                                lo_hi(p2l, lev, 0)[:, 8 * g:8 * g + 8],
                                src.rearrange("p j (m w) -> p j m w", w=w),
                                mask.rearrange("p j (m w) -> p j m w", w=w), ALU.mult).then_inc(S["p2m"], 1)
                        else:
                            dve.tensor_tensor(p2[:, 8 * g:8 * g + 8, :], src, mask,
                                              ALU.mult).then_inc(S["p2m"], 1)
                    if lev == 0:
                        conv(2, it)
                    for g in range(2):
                        n = 2 * LEVELS * it + 2 * lev + g + 1
                        dve.wait_ge(S["zn"], n)
                        w = 1 << lev
                        dst = lo_hi(yt, lev, 1) if last else lo_hi(zt, lev, 0)
                        dst = dst[:, 8 * g:8 * g + 8]
                        dve.tensor_tensor(
                            dst, GW[g][0:R, 0:4 * R].rearrange("p (j m w) -> p j m w", j=8, w=w), dst,
                            ALU.add).then_inc(S["zadd"], 1)
                    if lev < 4:
                        conv(lev + 3, it)
                for g in range(4):
                    dve.wait_ge(S["ks"], 4 * it + g + 1)
                    if g == 0:
                        dve.wait_ge(S["item_out"], it * NS + N0 + NS - 1)
                    for j in range(4):
                        b = 4 * g + j
                        ins = dve.scalar_tensor_tensor(
                            out=vs[:, b, :], in0=KSB[g][0:R, j * HD:(j + 1) * HD],
                            scalar=sm[:, 5, b:b + 1], in1=vs[:, b, :], op0=ALU.mult, op1=ALU.add)
                    ins.then_inc(S["r"], 1)
                make_ksq(it + 1)
                for g in range(4):
                    dve.wait_ge(S["su"], 4 * it + g + 1)
                    for j in range(4):
                        b = 4 * g + j
                        ins = dve.scalar_tensor_tensor(
                            out=state[:, b, :], in0=state[:, b, :], scalar=sdec[:, b:b + 1],
                            in1=SUB[g][:, j * HD:(j + 1) * HD], op0=ALU.mult, op1=ALU.add)
                    ins.then_inc(S["state"], 1)
            scale_outputs(IT)

        @block.gpsimd
        def _(pool):
            def make_gtri(it):
                g = t["glog"][:, 0:B] if it is None else t["glog"][:, bass.ds((it + 1) * B, B)]
                pool.tensor_tensor(gtri[:, :, :], g.unsqueeze(2).to_broadcast([C, B, C]),
                                   t["tri"][:, :].unsqueeze(1).to_broadcast([C, B, C]),
                                   ALU.mult).then_inc(S["gtri"], 1)

            def make_dt(base, it):
                k = (FIRST if it is None else STREAM).index(("d", 0))
                pool.wait_ge(S["item_out"], base + k + 1)
                if it is not None:
                    pool.wait_ge(S["up"], 4 * (it + 1))
                pool.tensor_tensor(dt_[:, :, :, :], ed[0:R, :, :].unsqueeze(2).to_broadcast([R, B, NH + 1, C]),
                                   t["dmask"][:, :, :].unsqueeze(1).to_broadcast([R, B, NH + 1, C]),
                                   ALU.mult).then_inc(S["dt"], 1)

            def gate_outputs(n):
                pool.wait_ge(S["stored"], 16 * (n + 1))
                pool.wait_ge(S["t1"], n + 1)
                pool.tensor_tensor(og[:, :], rt[:, :], gate[:, :], ALU.mult).then_inc(S["og"], 1)

            make_gtri(None)
            make_dt(0, None)
            pool.memset(gate[:, :], 0.0).then_inc(S["gate"], 1)
            with pool.Fori(0, IT) as it:
                base = it * NS + N0
                pool.wait_ge(S["item"], it * NS + 1)
                pool.wait_ge(S["dsum"], it + 1)
                make_gtri(it)
                for g in range(2):
                    bs = slice(8 * g, 8 * g + 8)
                    pool.wait_ge(S["up"], 4 * it + 2 * g + 2)
                    pool.tensor_tensor(u0[:, bs, :], up[0:R, bs, 0:NH, :].rearrange("p b i c -> p b (i c)"),
                                       t["mask0"][:, :].unsqueeze(1).to_broadcast([R, 8, R]),
                                       ALU.mult).then_inc(S["u0"], 1)
                    pool.wait_ge(S["u0"], 2 * it + g + 1)
                    pool.tensor_tensor(yt[:, bs, :], u0[:, bs, :],
                                       ident[0:R, 0:R].unsqueeze(1).to_broadcast([R, 8, R]),
                                       ALU.add).then_inc(S["yi"], 1)
                pool.wait_ge(S["gate"], it + 1)
                gate_outputs(it)
                pool.wait_ge(S["og"], it + 1)
                pool.sem_inc(S["passed"], 1)
                pool.tensor_copy(gate[:, :], gate_n[:, :]).then_inc(S["gate"], 1)
                pool.tensor_tensor(qsq[:, :].rearrange("p (b c) -> p b c", c=C), kq[:, :, QT, :], kq[:, :, QT, :],
                                   ALU.mult).then_inc(S["qsq"], 1)
                pool.wait_ge(S["qsq"], 2 * it + 1)
                pool.sem_inc(S["passed"], 1)
                pool.tensor_scalar(qsq[:, :], qsq[:, :], RMS_EPS * HD * HD, None, ALU.mult
                                   ).then_inc(S["qsq"], 1)
                make_dt(base, it)
                pool.wait_ge(S["osq"], it + 1)
                pool.wait_ge(S["qsq"], 2 * (it + 1))
                pool.tensor_tensor(osq[:, :], osq[:, :], qsq[:, :], ALU.add).then_inc(S["oqs"], 1)
            pool.wait_ge(S["gate"], IT + 1)
            gate_outputs(IT)


def load_expert(sp, a, e, u):
    def one_of(w):
        return w[bass.ds(e, 1)]

    sp.dma_start(a["w1s"][:, u, :, :], one_of(a["w1"]).rearrange("a (k p) f -> p (a k) f", p=P)
                 ).then_inc(a["loaded"][u], 16)
    sp.dma_start(a["b1s"][:, u, :], one_of(a["b1"]).rearrange("a (f p) -> p (a f)", p=P),
                 allow_slow_non_contiguous=True).then_inc(a["loaded"][u], 16)
    sp.dma_start(a["w2s"][:, u, :, :], one_of(a["w2"]).rearrange("a (f p) d -> p (a f) d", p=P)
                 ).then_inc(a["loaded"][u], 16)
    sp.dma_start(a["b2s"][:, u, :], one_of(a["b2"]).to_broadcast([P, D])).then_inc(a["loaded"][u], 16)


def project_and_route(nc, k, ex, ident, wo, rms_weight, router_w, h_dram, o_dram, xe_dram, sem):
    G = 4
    NG = NT // G
    GT_ = G * P
    with ExitStack() as ctx:
        def sb(name, shape, dt=F32):
            return ctx.enter_context(nc.sbuf_tensor(name, shape, dt))
        wo_s = sb("wo_s", [P, H, D])
        rw = sb("rw", [P, 1])
        rt_w = sb("rt_w", [P, KD_, E])
        o_in = sb("o_in", [P, 2, H, GT_])
        h_in = sb("h_in", [P, 2, G, D])
        hs = sb("hs", [P, G, D])
        xc = sb("xc", [P, 2, G, D])
        sq = sb("c_sq", [P, G, D])
        xT = sb("xT", [P, KD_, GT_])
        st = sb("st", [P, 5, G])
        eps = sb("c_eps", [P, 1])
        lg = sb("lg", [P, G, E])
        expl = sb("ex", [P, G, E])
        oh = sb("oh", [P, G, E])
        ohb = sb("ohb", [P, G, E], BF16)
        tmp = sb("tmp", [P, G, E])
        sc = sb("sc", [P, 8, G])
        slot = sb("slot", [P, 2, G], I32)
        carry = sb("carry", [P, E])
        rank = sb("rank", [P, E])
        ebase = sb("ebase", [P, E])
        trash = sb("trash", [P, NT])
        trif = sb("trif", [P, P])
        onesf = sb("onesf", [P, P])
        trib = sb("trib", [P, P], BF16)
        onesb = sb("onesb", [P, P], BF16)
        pr = [ctx.enter_context(nc.psum_tensor(f"pr{u}", [P, G, D], F32)) for u in range(2)]
        tp = ctx.enter_context(nc.psum_tensor("tp", [P, KD_, 512], F32))
        lp = ctx.enter_context(nc.psum_tensor("lp", [P, 512], F32))
        cp = ctx.enter_context(nc.psum_tensor("cp", [P, 512], F32))

        s_w, s_rw = sem("c_w"), sem("c_rw")
        s_in = [sem(f"c_in{u}") for u in range(2)]
        s_scat, s_sent, s_passed = sem("c_scat"), sem("c_sent"), sem("c_passed")
        s_c, s_ws, s_pr, s_hs, s_keep, s_v = (sem("c_" + n) for n in ("c", "ws", "pr", "hs", "keep", "v"))
        s_cen, s_sq, s_var, s_sd, s_xn, s_tr, s_xt = (
            sem("c_" + n) for n in ("cen", "sqr", "var", "sd", "xn", "tr", "xt"))
        s_lg, s_ls, s_ex, s_oh, s_pos, s_slot = (
            sem("c_" + n) for n in ("lg", "ls", "ex", "oh", "pos", "slot"))
        h_v = h_dram.rearrange("(g j p) d -> g p j d", j=G, p=P)
        block = ctx.enter_context(nc.Block())

        def groups(eng, body):
            with eng.Fori(0, NG // 2 - 1) as i:
                for u in range(2):
                    body(i * 2 + u, u, True)
            for u in range(2):
                body(NG - 2 + u, u, u == 0)

        @block.sync
        def _(sp):
            sp.dma_start(wo_s[:, :, :], wo.rearrange("(h p) n -> p h n", h=H)).then_inc(s_w, 16)
            sp.dma_start(rw[:, :], rms_weight.unsqueeze(1)).then_inc(s_w, 16)

            def load(g, u):
                for hh in range(H):
                    src = o_dram[hh].rearrange("p (g b) t -> p g (b t)", b=GT_ // T)
                    sp.dma_start(o_in[:, u, hh, :], src[:, bass.ds(g, 1), :].rearrange(
                        "p a c -> p (a c)")).then_inc(s_in[u], 16)
                sp.dma_start(h_in[:, u, :, :], h_v[bass.ds(g, 1)].rearrange(
                    "a p j d -> (a p) j d")).then_inc(s_in[u], 16)

            load(0, 0)
            load(1, 1)
            for kk in range(KD_):
                sp.dma_start(rt_w[:, kk, :], router_w[:, kk * P:(kk + 1) * P].rearrange("e p -> p e"),
                             allow_slow_non_contiguous=True).then_inc(s_rw, 16)
            with sp.Fori(0, NG // 2 - 1) as i:
                for u in range(2):
                    sp.wait_ge(s_hs, i * 2 + (u + 3))
                    load(i * 2 + (u + 2), u)
            for u in range(2):
                load_expert(sp, ex, u, u)

        @block.gpsimd
        def _(pool):
            n = [0]

            def step(ins):
                n[0] += 1
                ins.then_inc(s_c, 1)
                pool.wait_ge(s_c, n[0])

            step(pool.memset(trif[:, :], 1.0))
            step(pool.affine_select(out=trif[:, :], in_=trif[:, :], compare_op=ALU.is_ge, fill=0.0, base=0,
                                    pattern=[[1, P]], channel_multiplier=-1))
            step(pool.iota(rank[:, :], [[-1, E]], base=E, channel_multiplier=0,
                           allow_small_or_imprecise_dtypes=True))
            step(pool.iota(ebase[:, :], [[CAP, E]], base=0, channel_multiplier=0,
                           allow_small_or_imprecise_dtypes=True))
            step(pool.iota(trash[:, :], [[P, NT]], base=TRASH, channel_multiplier=1,
                           allow_small_or_imprecise_dtypes=True))

            def body(g, u, more):
                pool.wait_ge(s_hs, g + 3)
                pool.sem_inc(s_passed, 1)
                pool.tensor_copy(k["h2"][:, bass.ds(g * G, G), :], hs[:, :, :]).then_inc(s_keep, 1)
                pool.wait_ge(s_slot, g + 1)
                pool.sem_inc(s_passed, 1)
                for j in range(G):
                    pool.indirect_dma_start(xe_dram, bass.IndirectOffsetOnAxis(ap=slot[:, u, j:j + 1], axis=0),
                                            xc[:, u, j, :], None).then_inc(s_scat, 16)
                pool.wait_ge(s_scat, g * (16 * G) + 16 * G)
                pool.sem_inc(s_sent, 1)

            groups(pool, body)

        @block.tensor
        def _(pe):
            def project(g, u, j, heads):
                if j == 0 and heads[0] == 0:
                    pe.wait_ge(s_in[u], GROUP_IN * (g // 2 + 1))
                    pe.wait_ge(s_hs, g + 1)
                for hh in heads:
                    mm = pe.matmul(pr[u][:, j, :], o_in[:, u, hh, j * P:(j + 1) * P], wo_s[:, hh, :],
                                   start=(hh == 0), stop=(hh == H - 1))
                if j == G - 1 and heads[-1] == H - 1:
                    mm.then_inc(s_pr, 1)

            GROUP_IN = 16 * (H + 1)
            pe.wait_ge(s_ws, 2)
            for j in range(G):
                project(0, 0, j, range(H))
            pe.wait_ge(s_rw, 16 * KD_)
            pe.wait_ge(s_v, 2)

            def body(g, u, more):
                def ahead(j, heads):
                    if more:
                        project(g + 1, 1 - u, j, heads)

                for j in range(G - 1):
                    ahead(j, range(H))
                pe.wait_ge(s_xn, g + 1)
                for kk in range(KD_):
                    for j in range(G):
                        mm = pe.transpose(tp[:, kk, j * P:(j + 1) * P], xc[:, u, j, kk * P:(kk + 1) * P],
                                          ident[:, :])
                mm.then_inc(s_tr, 1)
                ahead(G - 1, range(H - 4))
                pe.wait_ge(s_xt, g + 1)
                for j in range(G):
                    for kk in range(KD_):
                        mm = pe.matmul(lp[:, j * E:(j + 1) * E], xT[:, kk, j * P:(j + 1) * P], rt_w[:, kk, :],
                                       start=(kk == 0), stop=(kk == KD_ - 1))
                mm.then_inc(s_lg, 1)
                ahead(G - 1, range(H - 4, H))
                pe.wait_ge(s_oh, g + 1)
                for j in range(G):
                    for i in range(j + 1):
                        pe.matmul(cp[:, j * E:(j + 1) * E], (trib if i == j else onesb)[:, :], ohb[:, i, :],
                                  start=(i == 0), stop=(i == j))
                for i in range(G):
                    mm = pe.matmul(cp[:, G * E:(G + 1) * E], onesb[:, :], ohb[:, i, :],
                                   start=(i == 0), stop=(i == G - 1))
                mm.then_inc(s_pos, 1)

            groups(pe, body)

        @block.scalar
        def _(act):
            act.wait_ge(s_w, 32)
            for hh in range(H):
                ins = act.mul(wo_s[:, hh, :], wo_s[:, hh, :], rw[:, 0:1])
            ins.then_inc(s_ws, 1)
            act.wait_ge(s_ws, 2)

            def body(g, u, more):
                act.wait_ge(s_cen, g + 1)
                act.activation(sq[:, :, :], xc[:, u, :, :], ACT.Square).then_inc(s_sq, 1)
                act.wait_ge(s_var, g + 1)
                act.activation(st[:, 2, :], st[:, 1, :], ACT.Sqrt, bias=eps[:, :],
                               scale=1.0 / D).then_inc(s_sd, 1)
                act.wait_ge(s_tr, g + 1)
                act.copy(xT[:, :, :], tp[:, :, :]).then_inc(s_xt, 1)
                act.wait_ge(s_ls, g + 1)
                act.activation(expl[:, :, :], lg[:, :, :], ACT.Exp).then_inc(s_ex, 1)

            groups(act, body)

        @block.vector
        def _(dve):
            dve.sem_inc(s_hs, 2)
            dve.sem_inc(s_keep, 1)
            dve.sem_inc(s_sent, 2)
            dve.memset(eps[:, :], LN_EPS)
            dve.memset(onesf[:, :], 1.0)
            dve.memset(carry[:, :], 0.0)
            dve.drain().then_inc(s_ws, 1)
            dve.wait_ge(s_c, 5)
            dve.wait_ge(s_ws, 1)
            dve.tensor_copy(onesb[:, :], onesf[:, :]).then_inc(s_v, 1)
            dve.tensor_copy(trib[:, :], trif[:, :]).then_inc(s_v, 1)

            def bc(a, n):
                return a.unsqueeze(2).to_broadcast([P, G, n])

            NV = 21

            def body(g, u, more):
                m = [0]

                def step(ins):
                    m[0] += 1
                    ins.then_inc(s_v, 1)
                    dve.wait_ge(s_v, g * NV + (2 + m[0]))

                dve.wait_ge(s_pr, g + 1)
                dve.wait_ge(s_keep, g + 1)
                dve.wait_ge(s_in[u], 16 * (H + 1) * (g // 2 + 1))
                dve.tensor_tensor(hs[:, :, :], pr[u][:, :, :], h_in[:, u, :, :], ALU.add).then_inc(s_hs, 1)
                dve.wait_ge(s_hs, g + 3)
                step(dve.tensor_reduce(st[:, 0, :], hs[:, :, :], AX_X, ALU.add))
                step(dve.tensor_scalar(st[:, 0, :], st[:, 0, :], -1.0 / D, None, ALU.mult))
                dve.wait_ge(s_sent, g + 1)
                dve.tensor_tensor(xc[:, u, :, :], hs[:, :, :], bc(st[:, 0, :], D), ALU.add).then_inc(s_cen, 1)
                dve.wait_ge(s_sq, g + 1)
                dve.tensor_reduce(st[:, 1, :], sq[:, :, :], AX_X, ALU.add).then_inc(s_var, 1)
                dve.wait_ge(s_sd, g + 1)
                step(dve.reciprocal(st[:, 3, :], st[:, 2, :]))
                dve.tensor_tensor(xc[:, u, :, :], xc[:, u, :, :], bc(st[:, 3, :], D), ALU.mult).then_inc(s_xn, 1)
                dve.wait_ge(s_lg, g + 1)
                lgp = lp[:, 0:G * E].rearrange("p (j e) -> p j e", e=E)
                step(dve.tensor_reduce(sc[:, 0, :], lgp, AX_X, ALU.max))
                dve.tensor_tensor(lg[:, :, :], lgp, bc(sc[:, 0, :], E), ALU.subtract).then_inc(s_ls, 1)
                dve.wait_ge(s_ls, g + 1)
                rk = rank[:, :].unsqueeze(1).to_broadcast([P, G, E])
                step(dve.tensor_scalar(tmp[:, :, :], lg[:, :, :], 0.0, None, ALU.is_ge))
                step(dve.tensor_tensor(tmp[:, :, :], tmp[:, :, :], rk, ALU.mult))
                step(dve.tensor_reduce(sc[:, 1, :], tmp[:, :, :], AX_X, ALU.max))
                step(dve.tensor_tensor(oh[:, :, :], rk, bc(sc[:, 1, :], E), ALU.is_equal))
                dve.tensor_copy(ohb[:, :, :], oh[:, :, :]).then_inc(s_oh, 1)
                dve.wait_ge(s_ex, g + 1)
                step(dve.tensor_reduce(sc[:, 2, :], expl[:, :, :], AX_X, ALU.add))
                step(dve.reciprocal(sc[:, 3, :], sc[:, 2, :]))
                step(dve.tensor_tensor(tmp[:, :, :], oh[:, :, :], ebase[:, :].unsqueeze(1).to_broadcast([P, G, E]),
                                       ALU.mult))
                step(dve.tensor_reduce(sc[:, 4, :], tmp[:, :, :], AX_X, ALU.add))
                dve.wait_ge(s_pos, g + 1)
                step(dve.tensor_tensor(tmp[:, :, :], cp[:, 0:G * E].rearrange("p (j e) -> p j e", e=E),
                                       carry[:, :].unsqueeze(1).to_broadcast([P, G, E]), ALU.add))
                step(dve.tensor_tensor(carry[:, :], cp[:, G * E:(G + 1) * E], carry[:, :], ALU.add))
                step(dve.tensor_tensor(tmp[:, :, :], tmp[:, :, :], oh[:, :, :], ALU.mult))
                step(dve.tensor_reduce(sc[:, 5, :], tmp[:, :, :], AX_X, ALU.add))
                step(dve.tensor_scalar(sc[:, 6, :], sc[:, 5, :], float(CAP), None, ALU.is_le))
                dve.tensor_tensor(k["weight"][:, bass.ds(g * G, G)], sc[:, 3, :], sc[:, 6, :], ALU.mult)
                step(dve.tensor_scalar(sc[:, 7, :], sc[:, 5, :], float(CAP), -1.0, ALU.min, ALU.add))
                dve.tensor_tensor(k["slot"][:, bass.ds(g * G, G)], sc[:, 7, :], sc[:, 4, :], ALU.add)
                tr = trash[:, bass.ds(g * G, G)]
                step(dve.tensor_tensor(sc[:, 5, :], sc[:, 7, :], sc[:, 4, :], ALU.add))
                step(dve.tensor_tensor(sc[:, 5, :], sc[:, 5, :], tr, ALU.subtract))
                step(dve.tensor_tensor(sc[:, 5, :], sc[:, 5, :], sc[:, 6, :], ALU.mult))
                dve.tensor_tensor(slot[:, u, :], sc[:, 5, :], tr, ALU.add).then_inc(s_slot, 1)
                assert m[0] == NV, m[0]

            groups(dve, body)


def experts(nc, ex, ident, xe_dram, ye_dram, sem):
    JT = CAP // P
    FT = F // P
    HALF = CAP // 2
    with ExitStack() as ctx:
        def sb(name, shape, dt=F32):
            return ctx.enter_context(nc.sbuf_tensor(name, shape, dt))
        w1s, w2s, b1s, b2s = ex["w1s"], ex["w2s"], ex["b1s"], ex["b2s"]
        xe = sb("xe", [P, 2, JT, D])
        xT = sb("d_xT", [P, 2, KD_, CAP])
        hT = sb("hT", [P, FT, CAP])
        ye = sb("ye", [P, 2, JT, D])
        tp = ctx.enter_context(nc.psum_tensor("d_tp", [P, 2, 512], F32))
        hp = ctx.enter_context(nc.psum_tensor("hp", [P, 4, 512], F32))
        yp = ctx.enter_context(nc.psum_tensor("yp", [P, 2, 512], F32))
        s_in = [sem(f"d_in{u}") for u in range(2)]
        s_out = [sem(f"d_out{u}") for u in range(2)]
        s_w = ex["loaded"]
        s_tr, s_xt, s_h, s_g, s_y, s_ye = (sem("d_" + n) for n in ("tr", "xt", "h", "g", "y", "ye"))
        NL = 4 * 16
        NTR = KD_ * JT // 4
        NH2 = 2 * FT
        block = ctx.enter_context(nc.Block())

        @block.sync
        def _(sp):
            def load_rows(e, u):
                sp.dma_start(xe[:, u, :, :], xe_dram[bass.ds(e * CAP, CAP), :].rearrange(
                    "(j p) d -> p j d", p=P)).then_inc(s_in[u], 16)

            load_rows(0, 0)
            load_rows(1, 1)
            with sp.Fori(0, E // 2 - 1) as i:
                for u in range(2):
                    sp.wait_ge(s_tr, i * (2 * NTR) + (u + 1) * NTR)
                    load_rows(i * 2 + (u + 2), u)
                    sp.wait_ge(s_ye, i * (2 * JT) + ((u + 1) * JT + 2))
                    load_expert(sp, ex, i * 2 + (u + 2), u)

        @block.tensor
        def _(pe):
            def transpose_rows(e, u):
                pe.wait_ge(s_in[u], e // 2 * 16 + 16)
                for q in range(NTR):
                    pe.wait_ge(s_xt, e * NTR + (q + 1))
                    for j4 in range(4):
                        kk, j = divmod(4 * q + j4, JT)
                        mm = pe.transpose(tp[:, q % 2, j4 * P:(j4 + 1) * P],
                                          xe[:, u, j, kk * P:(kk + 1) * P], ident[:, :])
                    mm.then_inc(s_tr, 1)

            def expert(i, u, more):
                e = i * 2 + u
                pe.wait_ge(s_w[u], i * NL + NL)
                pe.wait_ge(s_xt, e * NTR + (NTR + 2))
                for f in range(FT):
                    for half in range(2):
                        q = 2 * f + half
                        pe.wait_ge(s_g, e * NH2 + (q + 1))
                        for kk in range(KD_):
                            mm = pe.matmul(hp[:, q % 4, 0:HALF], w1s[:, u, kk, f * P:(f + 1) * P],
                                           xT[:, u, kk, half * HALF:(half + 1) * HALF],
                                           start=(kk == 0), stop=(kk == KD_ - 1))
                        mm.then_inc(s_h, 1)
                if more:
                    transpose_rows(e + 1, 1 - u)
                pe.wait_ge(s_g, e * NH2 + (NH2 + 4))
                for j in range(JT):
                    pe.wait_ge(s_ye, e * JT + (j + 1))
                    for f in range(FT):
                        mm = pe.matmul(yp[:, j % 2, 0:D], hT[:, f, j * P:(j + 1) * P], w2s[:, u, f, :],
                                       start=(f == 0), stop=(f == FT - 1))
                    mm.then_inc(s_y, 1)

            transpose_rows(0, 0)
            with pe.Fori(0, E // 2 - 1) as i:
                for u in range(2):
                    expert(i, u, True)
            for u in range(2):
                expert(E // 2 - 1, u, u == 0)

        @block.scalar
        def _(act):
            act.sem_inc(s_g, 4)
            with act.Fori(0, E // 2) as i:
                for u in range(2):
                    e = i * 2 + u
                    for q in range(NH2):
                        f, half = divmod(q, 2)
                        act.wait_ge(s_h, e * NH2 + (q + 1))
                        act.activation(hT[:, f, half * HALF:(half + 1) * HALF], hp[:, q % 4, 0:HALF],
                                       ACT.Gelu, bias=b1s[:, u, f:f + 1]).then_inc(s_g, 1)
                    act.wait_ge(s_ye, e * JT + (JT + 2))
                    act.dma_start(ye_dram[bass.ds(e * CAP, CAP), :].rearrange("(j p) d -> p j d", p=P),
                                  ye[:, u, :, :]).then_inc(s_out[u], 16)
            for u in range(2):
                act.wait_ge(s_out[u], 16 * (E // 2 + 1))

        @block.vector
        def _(dve):
            dve.sem_inc(s_xt, 2)
            dve.sem_inc(s_ye, 2)
            for u in range(2):
                dve.sem_inc(s_out[u], 16)

            def evacuate_rows(e, u):
                xTf = xT[:, u, :, :].rearrange("p k r -> p (k r)")
                for q in range(NTR):
                    dve.wait_ge(s_tr, e * NTR + (q + 1))
                    dve.tensor_copy(xTf[:, q * 512:(q + 1) * 512], tp[:, q % 2, :]).then_inc(s_xt, 1)

            def expert(i, u, more):
                e = i * 2 + u
                if more:
                    evacuate_rows(e + 1, 1 - u)
                dve.wait_ge(s_w[u], i * NL + NL)
                dve.wait_ge(s_out[u], i * 16 + 16)
                for j in range(JT):
                    dve.wait_ge(s_y, e * JT + (j + 1))
                    dve.tensor_tensor(ye[:, u, j, :], yp[:, j % 2, 0:D], b2s[:, u, :], ALU.add
                                      ).then_inc(s_ye, 1)

            evacuate_rows(0, 0)
            with dve.Fori(0, E // 2 - 1) as i:
                for u in range(2):
                    expert(i, u, True)
            for u in range(2):
                expert(E // 2 - 1, u, u == 0)


def combine(nc, k, ye_dram, out, sem):
    Q = 4
    QN = NT // Q
    with ExitStack() as ctx:
        yr = ctx.enter_context(nc.sbuf_tensor("yr", [P, NT, D], F32))
        s_y = [sem(f"f_y{q}") for q in range(Q)]
        s_m, s_a, s_o = sem("f_m"), sem("f_a"), sem("f_o")
        out_v = out.rearrange("b (s p) d -> p (b s) d", p=P)
        block = ctx.enter_context(nc.Block())

        @block.gpsimd
        def _(pool):
            for j in range(NT):
                pool.indirect_dma_start(yr[:, j, :], None, ye_dram,
                                        bass.IndirectOffsetOnAxis(ap=k["slot"][:, j:j + 1], axis=0)
                                        ).then_inc(s_y[j // QN], 16)

        @block.vector
        def _(dve):
            for q in range(Q):
                qs = slice(q * QN, (q + 1) * QN)
                dve.wait_ge(s_y[q], 16 * QN)
                dve.tensor_tensor(yr[:, qs, :], yr[:, qs, :],
                                  k["weight"][:, qs].unsqueeze(2).to_broadcast([P, QN, D]),
                                  ALU.mult).then_inc(s_m, 1)
                dve.wait_ge(s_m, q + 1)
                dve.tensor_tensor(yr[:, qs, :], yr[:, qs, :], k["h2"][:, qs, :], ALU.add).then_inc(s_a, 1)

        @block.sync
        def _(sp):
            for q in range(Q):
                qs = slice(q * QN, (q + 1) * QN)
                sp.wait_ge(s_a, q + 1)
                sp.dma_start(out_v[:, qs, :], yr[:, qs, :]).then_inc(s_o, 16)
            sp.wait_ge(s_o, 16 * Q)


_INS = ['x', 'L0_tok_w', 'L0_attn_Wq', 'L0_attn_Wk', 'L0_attn_Wv', 'L0_attn_Wb', 'L0_attn_Wa',
        'L0_attn_A_log', 'L0_attn_dt_bias', 'L0_attn_conv_q', 'L0_attn_conv_k', 'L0_attn_conv_v',
        'L0_attn_Wg', 'L0_attn_rms_weight', 'L0_attn_Wo', 'L0_ffn_router_w', 'L0_ffn_w1', 'L0_ffn_b1',
        'L0_ffn_w2', 'L0_ffn_b2']


def kernel(**inputs):
    import numpy as np
    import concourse.bacc as bacc
    from concourse.bass_utils import run_bass_kernel_spmd

    nc = bacc.Bacc("TRN2", target_bir_lowering=False, num_devices=1)
    arrays, args = {}, []
    for name in _INS:
        a = np.ascontiguousarray(inputs[name])
        arrays[f"in_{name}"] = a
        args.append(nc.dram_tensor(f"in_{name}", a.shape, mybir.dt.from_np(a.dtype), kind="ExternalInput").ap())
    out = nc.dram_tensor("out_h", (B, T, D), F32, kind="ExternalOutput").ap()
    build(nc, *args, out)
    r = run_bass_kernel_spmd(nc, [arrays], core_ids=[0])
    return r.results[0]["out_h"]
```
